# Optimizing a Trainium2 kernel written in Bass

```python
import numpy as np
import jax
import jax.numpy as jnp

def _softmax(x, axis=-1):
    return jax.nn.softmax(x, axis=axis)

def _gelu(x):
    return jax.nn.gelu(x, approximate=True)

def _silu(x):
    return jax.nn.silu(x)

def _sigmoid(x):
    return jax.nn.sigmoid(x)

def _layernorm(x, axis=-1, eps=1e-05):
    m = jnp.mean(x, axis=axis, keepdims=True)
    v = jnp.var(x, axis=axis, keepdims=True)
    return (x - m) / jnp.sqrt(v + eps)

def _scatter_add(tgt, idx, src, axis=0):
    return tgt.at[idx].add(src)

def _segment_sum(src, seg, n):
    return jax.ops.segment_sum(src, seg, n)
kernel_name = 'mk_gps_d1_gnn_r8_92daee'

def setup_inputs(seed: int=0):
    np.random.seed(seed)
    _w = jnp.asarray

    def _rec_inputs():
        import jax
        import jax.numpy as jnp
        _gk = jax.random.key(seed)
        x = -0.0003713 + 1 * jax.random.normal(jax.random.fold_in(_gk, 1), (6250, 256), jnp.float32)
        src = jax.random.randint(jax.random.fold_in(_gk, 2), (200000,), 0, 6250, jnp.int32)
        dst = jnp.minimum((6250 * jax.random.uniform(jax.random.fold_in(_gk, 3), (200000,)) ** 2.0).astype(jnp.int32), 49999)
        _o = jnp.argsort(dst, stable=True)
        src = src[_o]
        dst = dst[_o]
        edge_attr_3 = -1.09012e-05 + 0.99985 * jax.random.normal(jax.random.fold_in(_gk, 11), (200000, 3), jnp.float32)
        return (x, src, dst, edge_attr_3)
    x, src, dst, edge_attr_3 = _rec_inputs()

    def _L0_gnn_setup():
        import jax, jax.numpy as jnp
        import numpy as np
        N = 6250
        E = 50000
        IN = 256
        H = 8
        D = 32
        EF = 3
        key = jax.random.key(seed)
        ks = jax.random.split(key, 8)
        x = jax.random.normal(ks[0], (N, IN), dtype=jnp.float32)
        edge_index = jax.random.randint(ks[1], (2, E), 0, N, dtype=jnp.int64)
        edge_attr = jax.random.normal(ks[2], (E, EF), dtype=jnp.float32)
        W = jax.random.normal(ks[3], (H * D, IN), dtype=jnp.float32) * np.float32(np.sqrt(2.0 / (IN + H * D)))
        a_src = jax.random.normal(ks[4], (H, D), dtype=jnp.float32) * np.float32(np.sqrt(2.0 / (H + D)))
        a_dst = jax.random.normal(ks[5], (H, D), dtype=jnp.float32) * np.float32(np.sqrt(2.0 / (H + D)))
        edge_W = jax.random.normal(ks[6], (H * D, EF), dtype=jnp.float32) * np.float32(np.sqrt(2.0 / (EF + H * D)))
        edge_b = jnp.zeros((H * D,), dtype=jnp.float32)
        bias = jnp.zeros((H * D,), dtype=jnp.float32)
        return {'x': x, 'W': W, 'a_src': a_src, 'a_dst': a_dst, 'edge_W': edge_W, 'edge_b': edge_b, 'bias': bias, 'edge_attr': edge_attr, 'edge_index': edge_index}
    _L0_gnn_all = _L0_gnn_setup()
    _L0_gnn_in = {k: v for k, v in _L0_gnn_all.items() if k in ('W', 'a_src', 'a_dst', 'edge_W', 'edge_b', 'bias')}
    del _L0_gnn_all

    def _L0_mix_setup():
        import jax, jax.numpy as jnp
        import numpy as np
        D_MODEL = 256
        NHEAD = 8
        D_HEAD = D_MODEL // NHEAD
        DIM_FF = 1024
        B, L = (4, 2048)
        LN_EPS = 1e-05

        def _layernorm(x, g, b):
            mu = jnp.mean(x, axis=-1, keepdims=True)
            var = jnp.mean((x - mu) ** 2, axis=-1, keepdims=True)
            return (x - mu) * jax.lax.rsqrt(var + LN_EPS) * g + b

        def _phi(x):
            return jnp.where(x > 0, x + 1.0, jnp.exp(x))
        key = jax.random.key(seed)
        ks = jax.random.split(key, 16)
        s_in = 1.0 / np.sqrt(D_MODEL)
        s_ff = 1.0 / np.sqrt(DIM_FF)
        inp = {'x': jax.random.normal(ks[0], (B, L, D_MODEL), dtype=jnp.float32), 'Wq': jax.random.normal(ks[1], (D_MODEL, D_MODEL), dtype=jnp.float32) * s_in, 'bq': jnp.zeros((D_MODEL,), jnp.float32), 'Wk': jax.random.normal(ks[2], (D_MODEL, D_MODEL), dtype=jnp.float32) * s_in, 'bk': jnp.zeros((D_MODEL,), jnp.float32), 'Wv': jax.random.normal(ks[3], (D_MODEL, D_MODEL), dtype=jnp.float32) * s_in, 'bv': jnp.zeros((D_MODEL,), jnp.float32), 'Wo': jax.random.normal(ks[4], (D_MODEL, D_MODEL), dtype=jnp.float32) * s_in, 'bo': jnp.zeros((D_MODEL,), jnp.float32), 'W1': jax.random.normal(ks[5], (D_MODEL, DIM_FF), dtype=jnp.float32) * s_in, 'b1': jnp.zeros((DIM_FF,), jnp.float32), 'W2': jax.random.normal(ks[6], (DIM_FF, D_MODEL), dtype=jnp.float32) * s_ff, 'b2': jnp.zeros((D_MODEL,), jnp.float32), 'ln1_g': jnp.ones((D_MODEL,), jnp.float32), 'ln1_b': jnp.zeros((D_MODEL,), jnp.float32), 'ln2_g': jnp.ones((D_MODEL,), jnp.float32), 'ln2_b': jnp.zeros((D_MODEL,), jnp.float32)}
        return inp
    _L0_mix_all = _L0_mix_setup()
    _L0_mix_in = {k: v for k, v in _L0_mix_all.items() if k in ('Wq', 'bq', 'Wk', 'bk', 'Wv', 'bv', 'Wo', 'bo', 'W1', 'b1', 'W2', 'b2', 'ln1_g', 'ln1_b', 'ln2_g', 'ln2_b')}
    del _L0_mix_all

    def _L0_ffn_setup():
        import jax, jax.numpy as jnp
        import numpy as np
        C = 256
        HID = 1024
        E = 8
        TEMP = 1.0
        key = jax.random.key(seed)
        ks = jax.random.split(key, 7)
        x = jax.random.normal(ks[0], (8, 2048, C), dtype=jnp.float32)
        W1 = jax.random.normal(ks[1], (C, HID), dtype=jnp.float32) * 0.02
        b1 = jnp.zeros((HID,), dtype=jnp.float32)
        Wg = jax.random.normal(ks[2], (HID, E), dtype=jnp.float32) * 0.02
        bg = jnp.zeros((E,), dtype=jnp.float32)
        Wd = jax.random.normal(ks[3], (E, HID, C), dtype=jnp.float32) * 0.02
        bd = jnp.zeros((E, C), dtype=jnp.float32)
        return {'x': x, 'W1': W1, 'b1': b1, 'Wg': Wg, 'bg': bg, 'Wd': Wd, 'bd': bd}
    _L0_ffn_all = _L0_ffn_setup()
    _L0_ffn_in = {k: v for k, v in _L0_ffn_all.items() if k in ('W1', 'b1', 'Wg', 'bg', 'Wd', 'bd')}
    del _L0_ffn_all
    return {'x': x, 'src': src, 'dst': dst, 'edge_attr_3': edge_attr_3, 'L0_gnn_W': _L0_gnn_in['W'], 'L0_gnn_a_src': _L0_gnn_in['a_src'], 'L0_gnn_a_dst': _L0_gnn_in['a_dst'], 'L0_gnn_edge_W': _L0_gnn_in['edge_W'], 'L0_gnn_edge_b': _L0_gnn_in['edge_b'], 'L0_gnn_bias': _L0_gnn_in['bias'], 'L0_mix_Wq': _L0_mix_in['Wq'], 'L0_mix_bq': _L0_mix_in['bq'], 'L0_mix_Wk': _L0_mix_in['Wk'], 'L0_mix_bk': _L0_mix_in['bk'], 'L0_mix_Wv': _L0_mix_in['Wv'], 'L0_mix_bv': _L0_mix_in['bv'], 'L0_mix_Wo': _L0_mix_in['Wo'], 'L0_mix_bo': _L0_mix_in['bo'], 'L0_mix_W1': _L0_mix_in['W1'], 'L0_mix_b1': _L0_mix_in['b1'], 'L0_mix_W2': _L0_mix_in['W2'], 'L0_mix_b2': _L0_mix_in['b2'], 'L0_mix_ln1_g': _L0_mix_in['ln1_g'], 'L0_mix_ln1_b': _L0_mix_in['ln1_b'], 'L0_mix_ln2_g': _L0_mix_in['ln2_g'], 'L0_mix_ln2_b': _L0_mix_in['ln2_b'], 'L0_ffn_W1': _L0_ffn_in['W1'], 'L0_ffn_b1': _L0_ffn_in['b1'], 'L0_ffn_Wg': _L0_ffn_in['Wg'], 'L0_ffn_bg': _L0_ffn_in['bg'], 'L0_ffn_Wd': _L0_ffn_in['Wd'], 'L0_ffn_bd': _L0_ffn_in['bd']}

def reference(x, src, dst, edge_attr_3, L0_gnn_W, L0_gnn_a_src, L0_gnn_a_dst, L0_gnn_edge_W, L0_gnn_edge_b, L0_gnn_bias, L0_mix_Wq, L0_mix_bq, L0_mix_Wk, L0_mix_bk, L0_mix_Wv, L0_mix_bv, L0_mix_Wo, L0_mix_bo, L0_mix_W1, L0_mix_b1, L0_mix_W2, L0_mix_b2, L0_mix_ln1_g, L0_mix_ln1_b, L0_mix_ln2_g, L0_mix_ln2_b, L0_ffn_W1, L0_ffn_b1, L0_ffn_Wg, L0_ffn_bg, L0_ffn_Wd, L0_ffn_bd):
    import jax
    import jax.numpy as jnp

    def _L0_gnn_ref(x, W, a_src, a_dst, edge_W, edge_b, bias, edge_attr, edge_index):
        import jax, jax.numpy as jnp
        import numpy as np
        N = 6250
        E = 50000
        IN = 256
        H = 8
        D = 32
        EF = 3
        n = x.shape[0]
        h = (x @ W.T).reshape(n, H, D)
        src, dst = (edge_index[0], edge_index[1])
        h_src = h[src]
        h_dst = h[dst]
        alpha = jnp.einsum('ehd,hd->eh', h_src, a_src) + jnp.einsum('ehd,hd->eh', h_dst, a_dst)
        enc = jax.nn.relu(edge_attr @ edge_W.T + edge_b).reshape(-1, H, D)
        alpha = alpha + jnp.sum(enc * h_dst, axis=-1)
        alpha = jnp.where(alpha >= 0, alpha, 0.2 * alpha)
        amax = jax.ops.segment_max(alpha, dst, num_segments=n)
        ex = jnp.exp(alpha - amax[dst])
        denom = jax.ops.segment_sum(ex, dst, num_segments=n)
        attn = ex / jnp.maximum(denom[dst], 1e-10)
        out = jax.ops.segment_sum(h_src * attn[..., None], dst, num_segments=n)
        return out.reshape(n, H * D) + bias

    def _L0_mix_ref(x, Wq, bq, Wk, bk, Wv, bv, Wo, bo, W1, b1, W2, b2, ln1_g, ln1_b, ln2_g, ln2_b):
        import jax, jax.numpy as jnp
        import numpy as np
        D_MODEL = 256
        NHEAD = 8
        D_HEAD = D_MODEL // NHEAD
        DIM_FF = 1024
        B, L = (4, 2048)
        LN_EPS = 1e-05

        def _layernorm(x, g, b):
            mu = jnp.mean(x, axis=-1, keepdims=True)
            var = jnp.mean((x - mu) ** 2, axis=-1, keepdims=True)
            return (x - mu) * jax.lax.rsqrt(var + LN_EPS) * g + b

        def _phi(x):
            return jnp.where(x > 0, x + 1.0, jnp.exp(x))
        Bq, Lq, _ = x.shape
        q = (x @ Wq + bq).reshape(Bq, Lq, NHEAD, D_HEAD)
        k = (x @ Wk + bk).reshape(Bq, Lq, NHEAD, D_HEAD)
        v = (x @ Wv + bv).reshape(Bq, Lq, NHEAD, D_HEAD)
        q_phi = _phi(q)
        k_phi = _phi(k)
        kv = jnp.einsum('blhd,blhe->bhde', k_phi, v)
        k_sum = k_phi.sum(axis=1)
        z = 1.0 / (jnp.einsum('blhd,bhd->blh', q_phi, k_sum) + 1e-06)
        out = jnp.einsum('blhd,bhde,blh->blhe', q_phi, kv, z)
        out = out.reshape(Bq, Lq, D_MODEL) @ Wo + bo
        x = _layernorm(x + out, ln1_g, ln1_b)
        ff = jax.nn.relu(x @ W1 + b1) @ W2 + b2
        x = _layernorm(x + ff, ln2_g, ln2_b)
        return x

    def _L0_ffn_ref(x, W1, b1, Wg, bg, Wd, bd):
        import jax, jax.numpy as jnp
        import numpy as np
        C = 256
        HID = 1024
        E = 8
        TEMP = 1.0
        orig_shape = x.shape
        xf = x.reshape(-1, orig_shape[-1])
        H = jax.nn.gelu(xf @ W1 + b1, approximate=False)
        probs = jax.nn.softmax((H @ Wg + bg) / TEMP, axis=-1)
        assign = jnp.argmax(probs, axis=-1)
        out = jnp.zeros_like(xf)
        for e in range(Wd.shape[0]):
            y = H @ Wd[e] + bd[e]
            sel = (assign == e)[:, None]
            out = out + jnp.where(sel, probs[:, e:e + 1] * y, 0.0)
        return out.reshape(orig_shape)
    edge_index = jnp.stack([src, dst])
    xn = _layernorm(x, axis=-1)
    x = x + _L0_gnn_ref(xn, L0_gnn_W, L0_gnn_a_src, L0_gnn_a_dst, L0_gnn_edge_W, L0_gnn_edge_b, L0_gnn_bias, edge_attr_3, edge_index) + _L0_mix_ref(xn[None], L0_mix_Wq, L0_mix_bq, L0_mix_Wk, L0_mix_bk, L0_mix_Wv, L0_mix_bv, L0_mix_Wo, L0_mix_bo, L0_mix_W1, L0_mix_b1, L0_mix_W2, L0_mix_b2, L0_mix_ln1_g, L0_mix_ln1_b, L0_mix_ln2_g, L0_mix_ln2_b)[0]
    x = x + _L0_ffn_ref(_layernorm(x, axis=-1)[None], L0_ffn_W1, L0_ffn_b1, L0_ffn_Wg, L0_ffn_bg, L0_ffn_Wd, L0_ffn_bd)[0]
    return x

_drawn_inputs = setup_inputs


def setup_inputs(seed=0):
    import zlib

    import numpy as np

    out = dict(_drawn_inputs(seed))
    spreads = {'L0_gnn_edge_b': (0.0, 0.281),
     'L0_gnn_bias': (0.0, 0.1),
     'L0_mix_bq': (0.0, 0.8),
     'L0_mix_bk': (0.0, 0.8),
     'L0_mix_bv': (0.0, 0.1),
     'L0_mix_bo': (0.0, 0.1),
     'L0_mix_b1': (0.0, 0.1),
     'L0_mix_b2': (0.0, 0.1),
     'L0_mix_ln1_g': (1.0, 0.2),
     'L0_mix_ln1_b': (0.0, 0.1),
     'L0_mix_ln2_g': (1.0, 0.2),
     'L0_mix_ln2_b': (0.0, 0.1),
     'L0_ffn_b1': (0.0, 0.8),
     'L0_ffn_bg': (0.0, 0.8),
     'L0_ffn_bd': (0.0, 0.8)}
    factors = {'L0_mix_Wq': 8.0,
     'L0_mix_Wk': 8.0,
     'L0_mix_Wv': 7.672,
     'L0_ffn_W1': 5.203,
     'L0_ffn_Wg': 5.47,
     'L0_ffn_Wd': 6.408}
    for name, (base, spread) in spreads.items():
        noise = np.random.default_rng([zlib.crc32(name.encode()), seed]).standard_normal(out[name].shape)
        drawn = base * np.exp(spread * noise) if base else spread * noise
        out[name] = jnp.asarray(drawn.astype(out[name].dtype))
    for name, factor in factors.items():
        out[name] = (out[name] * factor).astype(out[name].dtype)
    return out
```

```python
from contextlib import ExitStack

import concourse.bass as bass
from concourse import mybir

F32 = mybir.dt.float32
BF16 = mybir.dt.bfloat16
I32 = mybir.dt.int32
ALU = mybir.AluOpType
ACT = mybir.ActivationFunctionType
X = mybir.AxisListType.X
ds = bass.ds

N, C, H, D, FF, NE = 6250, 256, 8, 32, 1024, 8
E = 200000
P = 125
T = N // P
SB = T // 2
W2T = 2 * P
KC = C // 128
JF = FF // 128
SE = 512
NS_USED = -(-E // SE)
NCH = 1568
NS = NCH // 4
EP = NCH * 128
ROWS = 16
BLK = NCH // ROWS
RL = EP // ROWS
ITEMS = NS_USED + T - 1
IB = 4
JI = ITEMS // IB
assert JI * IB == ITEMS
ITP = 448
HR = 8 + C
HW = C + 8
GB = 4
NT2 = (N + NE * 127) // 128
SROW = C + 4
BIG = 1e30
PAD_NODE = 8191
EPS = 1e-5
COMBO = [(0, 0), (0, 1), (0, 2), (1, 0), (1, 1), (1, 2), (2, 0), (2, 1)]
VECS = ["L0_mix_bo", "L0_mix_b2", "L0_mix_ln1_g", "L0_mix_ln1_b", "L0_mix_ln2_g", "L0_mix_ln2_b", "L0_gnn_bias"]


def wait(eng, sem, value):
    if isinstance(value, int) and value <= 0:
        return
    eng.wait_ge(sem, value)


def pipelined(eng, n, stages):
    top = max(lag for lag, _ in stages)

    def step(s):
        for lag, fn in stages:
            if not isinstance(s, int) or 0 <= s - lag < n:
                fn(s - lag)

    for s in range(top + 1):
        step(s)
    with eng.Fori(top + 1, n) as s:
        step(s)
    for s in range(n, n + top):
        step(s)


def build_program(nc, io):
    stack = ExitStack()
    with stack:
        def sem(name):
            return stack.enter_context(nc.semaphore(name))

        def sems(name, n=2):
            return [sem(f"{name}{i}") for i in range(n)]

        def sb(name, shape, dt=F32, at=stack):
            return at.enter_context(nc.sbuf_tensor(name, shape, dt))

        bank = [stack.enter_context(nc.psum_tensor(f"bank{i}", [128, 512], F32)) for i in range(8)]

        h_tab = nc.dram_tensor("h_tab", (N, HR), F32).ap()
        hsplit = nc.dram_tensor("hsplit", (T, P, 3 * HW), BF16).ap()
        attrx = nc.dram_tensor("attrx", (24, EP), BF16).ap()
        spill = nc.dram_tensor("spill", (NS, 128, 4 * C), F32).ap()
        accd = nc.dram_tensor("accd", (N, C), F32).ap()
        routed = nc.dram_tensor("routed", (NT2 * 128, SROW), F32).ap()

        ident = sb("ident", [128, 128])
        r1 = sb("r1", [128, T * C])
        al = sb("al", [128, NCH * H])
        items = sb("items", [1, 2 * ITP], I32)
        nid = sb("nid", [128, T])
        eps_c = sb("eps_c", [128, 1])
        zrow = sb("zrow", [1, 132])
        ew_bf = sb("ew_bf", [32, C], BF16)
        al3 = al[:, :].rearrange("p (c h) -> p c h", h=H)
        ad = r1[:, 0:NCH * H]
        ad3 = ad.rearrange("p (c h) -> p c h", h=H)

        gather_mem = ExitStack()
        src_t = sb("src_t", [128, NCH], I32, gather_mem)
        mem_setup = ExitStack()
        ewf = sb("ewf", [32, C], at=mem_setup)
        ewr = sb("ewr", [32, C], at=mem_setup)
        ewp = sb("ewp", [32, 3, C], BF16, mem_setup)
        ewm = sb("ewm", [32, 3], at=mem_setup)
        lastb = sb("lastb", [64, ITP], at=mem_setup)
        thr = sb("thr", [64, 3], at=mem_setup)
        cnt = sb("cnt", [64, 2], at=mem_setup)
        iota_i = sb("iota_i", [64, ITP], at=mem_setup)
        itf = sb("itf", [1, 2 * ITP], at=mem_setup)
        ones_s = sb("ones_s", [1, 64], at=mem_setup)
        dlast_i = sb("dlast_i", [1, NS], I32, mem_setup)
        dlast = sb("dlast", [1, NS], at=mem_setup)
        fill = sb("fill", [128, SROW], at=mem_setup)
        mem_setup.close()
        gbuf = [sb(f"gbuf{b}", [128, 4, HR], at=gather_mem) for b in range(GB)]
        gidx = [sb(f"gidx{b}", [128, 4], I32, gather_mem) for b in range(GB)]

        consts_in, x_in, wa_in, edges_in = sem("consts_in"), sem("x_in"), sem("wa_in"), sem("edges_in")
        prep, own_step = sem("prep"), sem("own_step")
        items_ready, attr_stored, routed_filled, fill_ready = sem("items_ready"), sem("attr_stored"), sem("routed_filled"), sem("fill_ready")
        setup_mm, setup_ev = sem("setup_mm"), sem("setup_ev")

        mem_ab = ExitStack()
        xt = sb("xt", [P, T, C], at=mem_ab)
        mem_a = ExitStack()
        wg = sb("wg", [128, KC, C], at=mem_a)
        abd = sb("abd", [128, KC, 16], at=mem_a)
        wh = sb("wh", [128, KC, 8 + C + 8], at=mem_a)
        wkv = sb("wkv", [128, KC, 2 * C], at=mem_a)
        bkv = sb("bkv", [P, 2 * C], at=mem_a)
        xs = [sb(f"xs{u}", [P, C], at=mem_a) for u in range(2)]
        xT = [sb(f"xT{u}", [128, KC, P], at=mem_a) for u in range(2)]
        hs = [sb(f"hs{u}", [P, 8 + C + 8], at=mem_a) for u in range(2)]
        hrest = [sb(f"hrest{u}", [P, HW], at=mem_a) for u in range(2)]
        hb = [sb(f"hb{u}", [P, 3, HW], BF16, mem_a) for u in range(2)]
        kvb = [sb(f"kvb{u}", [P, C + 2 * 129], at=mem_a) for u in range(2)]
        ek = [sb(f"ek{u}", [P, C], at=mem_a) for u in range(2)]
        kphi = [sb(f"kphi{u}", [P, C], at=mem_a) for u in range(2)]
        xsum, xvar = sb("xsum", [P, T], at=mem_a), sb("xvar", [P, T], at=mem_a)
        mem_a.close()
        mem_b = ExitStack()
        wq = sb("wq", [128, KC, C], at=mem_b)
        bq = sb("bq", [128, KC], at=mem_b)
        wo = sb("wo", [128, KC, C], at=mem_b)
        vec = sb("vec", [128, len(VECS), C], at=mem_b)
        kvm = sb("kvm", [128, 132], at=mem_b)
        kvr = sb("kvr", [128, KC, 132], at=mem_b)
        b1m = sb("b1m", [128, JF], at=mem_b)
        mem_b1 = ExitStack()
        eq = sb("eq", [128, KC, W2T], at=mem_b1)
        rq = sb("rq", [128, KC, W2T], at=mem_b1)
        qphi = sb("qphi", [128, KC, W2T], at=mem_b1)
        den = [sb(f"den{u}", [P, 2, H], at=mem_b1) for u in range(2)]
        at = [sb(f"at{u}", [P, C], at=mem_b1) for u in range(2)]
        atT = sb("atT", [128, 2, KC, P], at=mem_b1)
        y1t = [sb(f"y1t{u}", [P, C], at=mem_b1) for u in range(2)]
        mem_b1.close()
        mem_b3 = ExitStack()
        st = [sb(f"st{u}", [P, 2, 6], at=mem_b3) for u in range(2)]
        mv = [sb(f"mv{u}", [P, 2, 2], at=mem_b3) for u in range(2)]
        sd = [sb(f"sd{u}", [P, 2, 2], at=mem_b3) for u in range(2)]
        yn = [sb(f"yn{u}", [P, C], at=mem_b3) for u in range(2)]
        y2 = [sb(f"y2{u}", [P, C], at=mem_b3) for u in range(2)]
        ac = sb("ac", [P, 2, C], at=mem_b3)
        xr = sb("xr", [P, 2, C], at=mem_b3)
        mem_b3.close()
        w1m = r1[:, 0:KC * FF].rearrange("p (k f) -> p k f", k=KC)
        w2m = r1[:, KC * FF:KC * FF + JF * C].rearrange("p (j c) -> p j c", j=JF)
        f1 = r1[:, 4096:4096 + JF * W2T].rearrange("p (j n) -> p j n", j=JF)
        ynT = r1[:, 6400:6400 + KC * W2T].rearrange("p (k n) -> p k n", k=KC)
        mem_b.close()
        mem_ab.close()
        xnT = r1[:, 0:KC * N].rearrange("p (k n) -> p k n", k=KC)

        mem_e = ExitStack()
        dstb = [sb(f"dstb{b}", [P, SE], I32, mem_e) for b in range(IB)]
        att = [sb(f"att{b}", [32, SE], BF16, mem_e) for b in range(IB)]
        hbt = [sb(f"hbt{b}", [P, 3, HW], BF16, mem_e) for b in range(IB)]
        oneh_t = [sb(f"oneh_t{g}", [P, 256], BF16, mem_e) for g in range(2)]
        enc = [sb(f"enc{g}", [128, 2, C], at=mem_e) for g in range(2)]
        prod = [sb(f"prod{g}", [128, 2, C], at=mem_e) for g in range(2)]
        red = [sb(f"red{g}", [128, 2, H], at=mem_e) for g in range(2)]
        red2 = [sb(f"red2{g}", [128, 2, H], at=mem_e) for g in range(2)]
        mem_e.close()
        gather_mem.close()

        mem_s = ExitStack()
        bl = sb("bl", [128, RL], at=mem_s)
        sst = [sb(f"sst{u}", [128, 7 * 128], at=mem_s) for u in range(2)]
        edge_v = sb("edge_v", [128, 4], at=mem_s)
        rows = sb("rows", [1, 12, 128], at=mem_s)
        carry = sb("carry", [128, 2], at=mem_s)
        mem_s.close()
        dbi = al[:, 0:RL].bitcast(I32)
        run = al[:, 0:RL]
        flag = r1[:, 0:RL + 1]
        ex = r1[:, 0:NCH * H]
        ex3 = ex.rearrange("p (c h) -> p c h", h=H)

        mem_2 = ExitStack()
        acc = sb("acc", [P, T, HW], at=mem_2)
        msg = [sb(f"msg{g}", [128, 2, HW], at=mem_2) for g in range(2)]
        oneh = [sb(f"oneh{g}", [128, 2, P], at=mem_2) for g in range(2)]
        dst_i = sb("dst_i", [128, NCH], I32, mem_2)
        dst_f = sb("dst_f", [128, NCH], at=mem_2)
        hsb = [al[:, b * 4 * C:(b + 1) * 4 * C] for b in range(IB)]
        nidx = al[:, IB * 4 * C:IB * 4 * C + N]
        mem_d = ExitStack()
        xa = sb("xa", [P, 2, C], at=mem_d)
        dn = [sb(f"dn{u}", [P, 2, H], at=mem_d) for u in range(2)]
        ag = [sb(f"ag{u}", [P, C], at=mem_d) for u in range(2)]
        dst_6 = [sb(f"dst_6{u}", [P, 6], at=mem_d) for u in range(2)]
        dmv = [sb(f"dmv{u}", [P, 2], at=mem_d) for u in range(2)]
        pack = sb("pack", [P, T, 4], at=mem_d)
        lg = sb("lg", [P, T, NE], at=mem_d)
        pos_i = sb("pos_i", [P, T], I32, mem_d)
        e_row = sb("e_row", [1, 64], I32, mem_d)
        rt = [sb(f"rt{i}", [P, T * NE], at=mem_d) for i in range(6)]
        rs = [sb(f"rs{i}", [P, 64], at=mem_d) for i in range(4)]
        rsi = sb("rsi", [P, 8], I32, mem_d)
        ejt = sb("ejt", [1, 64 * NE], at=mem_d)
        routec = sb("routec", [128, 125 + 125 + 400 + 8 + 64 + 1 + 50], at=mem_d)
        bg = sb("bg", [P, NE], at=mem_d)
        b1f = sb("b1f", [128, JF], at=mem_d)
        xd = [sb(f"xd{u}", [P, C], at=mem_d) for u in range(2)]
        srow = [sb(f"srow{u}", [P, SROW], at=mem_d) for u in range(2)]
        sidx = [sb(f"sidx{u}", [P, 1], I32, mem_d) for u in range(2)]
        mem_d.close()
        mem_2.close()
        x2 = r1[0:P, 0:T * C].rearrange("p (t c) -> p t c", t=T)
        w1f = al[:, 0:KC * FF].rearrange("p (k f) -> p k f", k=KC)
        wgt = al[:, 2048:2048 + JF * NE].rearrange("p (j e) -> p j e", j=JF)
        hT = al[:, 2176:2176 + JF * 256].rearrange("p (j n) -> p j n", j=JF)
        xdT = al[:, 4352:4352 + KC * 256].rearrange("p (k n) -> p k n", k=KC)
        bdr = al[0:1, 4864:4864 + NE * C]
        ones_r = al[0:1, 6912:6912 + 128]
        mem_x = ExitStack()
        wd = sb("wd", [128, NE, JF * C], at=mem_x)
        xg = [sb(f"xg{u}", [128, SROW], at=mem_x) for u in range(2)]
        xgn = [sb(f"xgn{u}", [128, C], at=mem_x) for u in range(2)]
        oidx = [sb(f"oidx{u}", [128, 1], I32, mem_x) for u in range(2)]
        og = [sb(f"og{u}", [128, C], at=mem_x) for u in range(2)]
        mem_x.close()

        sq_ready, sd_ready = sem("sq_ready"), sem("sd_ready")
        var_ready = sem("var_ready")
        xs_ready, xT_done, xT_ready, xnT_copied = sem("xs_ready"), sem("xT_done"), sem("xT_ready"), sem("xnT_copied")
        mm_done, hs_copied, h_stored, split_step, hb_stored = sem("mm_done"), sem("hs_copied"), sems("h_stored"), sem("split_step"), sems("hb_stored")
        kv_added, k_exped, k_pos, kphi_ready, kv_acc = sem("kv_added"), sem("k_exped"), sem("k_pos"), sem("kphi_ready"), sem("kv_acc")
        kv_summed = sem("kv_summed")
        pool_went_on, vec_went_on = sem("pool_went_on"), sem("vec_went_on")
        idx_staged, gathered, spilled, asrc_kept = sem("idx_staged"), sems("gathered", GB), sems("spilled", GB), sem("asrc_kept")
        wb_in, kvr_ready, wf_in = sem("wb_in"), sem("kvr_ready"), sem("wf_in")
        q_ready, q_exped, q_relu, qphi_ready = sem("q_ready"), sem("q_exped"), sem("q_relu"), sem("qphi_ready")
        n_ready, den_step, at_ready = sem("n_ready"), sems("den_step"), sem("at_ready")
        t_ready, atT_ready, o_ready, y1_read, y1_ready = sem("t_ready"), sem("atT_ready"), sem("o_ready"), sem("y1_read"), sem("y1_ready")
        ln1_var, ln1_sd, ln_step, yn_ready = sem("ln1_var"), sem("ln1_sd"), sems("ln_step"), sem("yn_ready")
        st_ready = sem("st_ready")
        yT_done, ynT_ready, f_mm, f_relu, g_ready = sem("yT_done"), sem("ynT_ready"), sem("f_mm"), sem("f_relu"), sem("g_ready")
        z_read, ln2_var, ln2_sd, ln2_step = sem("z_read"), sem("ln2_var"), sem("ln2_sd"), sems("ln2_step")
        st2_ready = sems("st2_ready")
        xr_in, acc_ready, acc_stored = sem("xr_in"), sem("acc_ready"), sem("acc_stored")
        item_in, oneh_t_ready, d_ready, enc_ready = sems("item_in", IB), sem("oneh_t_ready"), sem("d_ready"), sem("enc_ready")
        prod_ready, red_ready, d_read, ad_added, ad_zero = sem("prod_ready"), sem("red_ready"), sem("d_read"), sem("ad_added"), sem("ad_zero")
        att_ones = sem("att_ones")
        sst_ready, bt_ready, bl_copied = sem("sst_ready"), sem("bt_ready"), sem("bl_copied")
        dst_row_in, s_step, s_tr, s_trc = sem("dst_row_in"), sem("s_step"), sem("s_tr"), sem("s_trc")
        dif_ready, exp_ready, xt_ready, ex_copied = sem("dif_ready"), sem("exp_ready"), sem("xt_ready"), sem("ex_copied")
        nidx_in, hs_in, msg_ready, msgd_ready, acc_added = sem("nidx_in"), sems("hs_in", IB), sem("msg_ready"), sem("msgd_ready"), sem("acc_added")
        dstf_ready, acc_zero = sem("dstf_ready"), sem("acc_zero")
        m_used = sem("m_used")
        x2_aggr = sem("x2_aggr")
        xa_in, x2_step, x2_ready, dsd_ready, drs_ready = sem("xa_in"), sems("x2_step"), sem("x2_ready"), sem("dsd_ready"), sem("drs_ready")
        wr_in, xd_ready, xdt_done, xdT_ready, dh_mm, dh_gelu, lg_mm, lg_ready = sem("wr_in"), sem("xd_ready"), sem("xdt_done"), sem("xdT_ready"), sem("dh_mm"), sem("dh_gelu"), sem("lg_mm"), sem("lg_ready")
        r_step, r_exp, r_mm, route_ready = sem("r_step"), sem("r_exp"), sem("r_mm"), sem("route_ready")
        srow_ready, sidx_ready, scattered = sems("srow_ready"), sem("sidx_ready"), sems("scattered")
        wd_in, xg_in, xgn_ready, gT_done, gT_ready, gh_mm, gh_gelu, y_ready = sem("wd_in"), sems("xg_in"), sem("xgn_ready"), sem("gT_done"), sem("gT_ready"), sem("gh_mm"), sem("gh_gelu"), sem("y_ready")
        og_ready, oidx_ready, out_stored = sem("og_ready"), sem("oidx_ready"), sems("out_stored")

        x_t = io["x"].rearrange("(t p) c -> p t c", p=P)
        h_tab_t = h_tab.rearrange("(t p) c -> t p c", p=P)
        accd_t = accd.rearrange("(t p) c -> p t c", p=P)

        def item_reg(eng, which, i):
            top = [NS - 1, T - 1][which]
            return eng.value_load(items[0:1, ds(which * ITP + i, 1)], min_val=0, max_val=top)

        block = stack.enter_context(nc.Block())
        attr_f = al[:, 0:4704].rearrange("p (k j) -> p k j", k=3)
        attr_b = [al[:, 4704 + 2352 * n:4704 + 2352 * (n + 1)].bitcast(BF16).rearrange("p (k j) -> p k j", k=3) for n in range(3)]
        EJ = EP // 128

        @block.sync
        def _(sp):
            sp.dma_start(xt[:, :, :], x_t).then_inc(x_in, 16)
            sp.dma_start(wg[:, :, :], io["wg"]).then_inc(wa_in, 16)
            sp.dma_start(abd[:, :, :], io["abd"]).then_inc(wa_in, 16)
            sp.dma_start(wh[:, :, 8:8 + C], io["wgT"]).then_inc(wa_in, 16)
            sp.dma_start(wkv[:, :, :], io["wkv"]).then_inc(wa_in, 16)
            sp.dma_start(bkv[:, :], io["bkv"]).then_inc(wa_in, 16)
            sp.dma_start(attr_f, io["attr"].rearrange("k (p j) -> p k j", p=128)).then_inc(edges_in, 16)
            sp.wait_ge(prep, 3)
            for q, (part, _) in enumerate(COMBO):
                sp.dma_start(attrx[3 * q:3 * q + 3, :].rearrange("k (p j) -> p k j", p=128), attr_b[part]).then_inc(attr_stored, 16)
            sp.wait_ge(fill_ready, 2)
            sp.dma_start(routed.rearrange("(t p) c -> p t c", p=128),
                         fill[:, :].unsqueeze(1).to_broadcast([128, NT2, SROW])).then_inc(routed_filled, 16)
            with sp.Fori(0, SB) as i:
                for u in range(2):
                    sp.wait_ge(hs_copied, 2 * i + u + 1)
                    sp.dma_start(h_tab_t[ds(2 * i + u, 1)].rearrange("t p c -> p (t c)"), hs[u][:, 0:HR]).then_inc(h_stored[u], 16)
                for u in range(2):
                    sp.wait_ge(split_step, 10 * i + 5 * u + 5)
                    sp.dma_start(hsplit[ds(2 * i + u, 1)].rearrange("t p c -> p (t c)"), hb[u][:, :, :].rearrange("p a c -> p (a c)")).then_inc(hb_stored[u], 16)
            with sp.Fori(0, NS // GB) as j:
                for b in range(GB):
                    sp.wait_ge(gathered[b], 64 * j + 64)
                    sp.dma_start(spill[ds(GB * j + b, 1)].rearrange("s p (u c) -> p (s u) c", u=4), gbuf[b][:, :, 8:HR]).then_inc(spilled[b], 16)
            for b in range(GB):
                sp.wait_ge(spilled[b], 16 * (NS // GB))
            sp.wait_ge(bt_ready, 14)
            dst_rows = io["dst"].rearrange("(r j) -> r j", r=ROWS)
            for h in range(H):
                sp.dma_start(dbi[h:128:H, :], dst_rows).then_inc(dst_row_in, 16)
            sp.wait_ge(dif_ready, 14)
            sp.wait_ge(xt_ready, 14)
            sp.dma_start(dst_i[:, :], io["dst_t"]).then_inc(nidx_in, 16)
            sp.dma_start(nidx, io["node_row"].partition_broadcast(128)).then_inc(nidx_in, 16)

            def load_h(j, b):
                s = item_reg(sp, 0, IB * j + b)
                sp.dma_start(hsb[b], spill[ds(s, 1)].rearrange("s p c -> p (s c)")).then_inc(hs_in[b], 16)

            for b in range(IB):
                load_h(0, b)
            with sp.Fori(1, JI) as j:
                for b in range(IB):
                    sp.wait_ge(msg_ready, 2 * (IB * (j - 1) + b + 1))
                    load_h(j, b)
            sp.wait_ge(msg_ready, 2 * ITEMS)
            sp.wait_ge(m_used, 2 * ITEMS)
            sp.dma_start(w1f, io["w1f"]).then_inc(wr_in, 16)
            sp.dma_start(wgt, io["wgate"]).then_inc(wr_in, 16)
            sp.dma_start(bdr, io["bd"]).then_inc(wr_in, 16)
            sp.dma_start(ones_r, io["ones"]).then_inc(wr_in, 16)
            sp.dma_start(bg[:, :], io["bg"]).then_inc(wr_in, 16)
            sp.dma_start(b1f[:, :], io["b1f"]).then_inc(wr_in, 16)
            sp.dma_start(routec[:, :], io["routec"]).then_inc(wr_in, 16)

            def x2_load(i):
                wait(sp, x2_ready, 2 * i)
                sp.dma_start(xa[:, :, :], accd_t[:, ds(2 * i, 2), :]).then_inc(xa_in, 16)

            pipelined(sp, SB, [(0, x2_load)])
            for u in range(2):
                sp.wait_ge(scattered[u], 16 * SB)
            sp.dma_start(wd[:, :, :], io["wd"]).then_inc(wd_in, 16)

            def x_load(j):
                for u in range(2):
                    wait(sp, og_ready, 2 * j + u - 1)
                    wait(sp, oidx_ready, 2 * j + u - 1)
                    wait(sp, xgn_ready, 2 * j + u - 1)
                    sp.dma_start(xg[u][:, :], routed[ds((2 * j + u) * 128, 128), :]).then_inc(xg_in[u], 16)

            pipelined(sp, NT2 // 2, [(0, x_load)])
            for u in range(2):
                sp.wait_ge(out_stored[u], 16 * (NT2 // 2))

        @block.gpsimd
        def _(pool):
            pool.memset(fill[:, :], 0.0).then_inc(fill_ready, 1)
            pool.wait_ge(fill_ready, 1)
            pool.memset(fill[:, SROW - 1:SROW].bitcast(I32), PAD_NODE).then_inc(fill_ready, 1)

            def a_split(i):
                for u in range(2):
                    pool.wait_ge(xT_ready, 2 * i + u + 1)
                    pool.tensor_copy(xnT[:, :, ds((2 * i + u) * P, P)], xT[u][:, :, :]).then_inc(xnT_copied, 1)
                for u in range(2):
                    pool.wait_ge(hs_copied, 2 * i + u + 1)
                    wait(pool, hb_stored[u], 16 * i)
                    hn = hs[u][:, 8:8 + HW]
                    pool.sem_inc(pool_went_on, 1)
                    pool.tensor_copy(hb[u][:, 0, :], hn).then_inc(split_step, 1)
                    pool.wait_ge(split_step, 10 * i + 5 * u + 1)
                    pool.tensor_tensor(hrest[u][:, :], hn, hb[u][:, 0, :], ALU.subtract).then_inc(split_step, 1)
                    pool.wait_ge(split_step, 10 * i + 5 * u + 2)
                    pool.sem_inc(pool_went_on, 1)
                    pool.tensor_copy(hb[u][:, 1, :], hrest[u][:, :]).then_inc(split_step, 1)
                    pool.wait_ge(split_step, 10 * i + 5 * u + 3)
                    pool.tensor_tensor(hrest[u][:, :], hrest[u][:, :], hb[u][:, 1, :], ALU.subtract).then_inc(split_step, 1)
                    pool.wait_ge(split_step, 10 * i + 5 * u + 4)
                    pool.sem_inc(pool_went_on, 1)
                    pool.tensor_copy(hb[u][:, 2, :], hrest[u][:, :]).then_inc(split_step, 1)

            pipelined(pool, SB, [(0, a_split)])
            for u in range(2):
                pool.wait_ge(h_stored[u], 16 * SB)
            pool.wait_ge(attr_stored, 16 * len(COMBO))
            pool.wait_ge(edges_in, 32)
            pool.wait_ge(items_ready, 1)
            pool.wait_ge(routed_filled, 16)

            def keep_asrc(j, b):
                pool.wait_ge(gathered[b], 64 * j + 64)
                pool.tensor_copy(al3[:, ds(4 * (GB * j + b), 4), :], gbuf[b][:, :, 0:8]).then_inc(asrc_kept, 1)

            def gather(j, b):
                wait(pool, spilled[b], 16 * j)
                wait(pool, asrc_kept, 0 if isinstance(j, int) else GB * (j - 1) + b + 1)
                pool.tensor_copy(gidx[b][:, :], src_t[:, ds(4 * (GB * j + b), 4)]).then_inc(idx_staged, 1)
                pool.wait_ge(idx_staged, GB * j + b + 1)
                pool.sem_inc(pool_went_on, 1)
                for c in range(4):
                    pool.indirect_dma_start(gbuf[b][:, c, :], None, h_tab, bass.IndirectOffsetOnAxis(ap=gidx[b][:, c:c + 1], axis=0)).then_inc(gathered[b], 16)

            for b in range(GB):
                gather(0, b)
            with pool.Fori(1, NS // GB) as j:
                for b in range(GB):
                    keep_asrc(j - 1, b)
                    gather(j, b)
            for b in range(GB):
                keep_asrc(NS // GB - 1, b)
            pool.wait_ge(ex_copied, 14)
            pool.memset(acc[:, :, :], 0.0).then_inc(acc_zero, 1)
            pool.wait_ge(route_ready, 1)

            def scatter(i):
                for u in range(2):
                    wait(pool, scattered[u], 16 * i)
                    pool.tensor_copy(sidx[u][:, :], pos_i[:, ds(2 * i + u, 1)]).then_inc(sidx_ready, 1)
                for u in range(2):
                    pool.wait_ge(srow_ready[u], 2 * i + 2)
                    pool.wait_ge(sidx_ready, 2 * i + u + 1)
                    pool.sem_inc(pool_went_on, 1)
                    pool.indirect_dma_start(routed, bass.IndirectOffsetOnAxis(ap=sidx[u][:, 0:1], axis=0), srow[u][:, :], None).then_inc(scattered[u], 16)

            pipelined(pool, SB, [(0, scatter)])

            def x_store(j):
                for u in range(2):
                    pool.wait_ge(xg_in[u], 16 * j + 16)
                    wait(pool, out_stored[u], 16 * j)
                    pool.sem_inc(pool_went_on, 1)
                    pool.tensor_copy(oidx[u][:, :], xg[u][:, SROW - 1:SROW].bitcast(I32)).then_inc(oidx_ready, 1)
                for u in range(2):
                    pool.wait_ge(og_ready, 2 * j + u + 1)
                    pool.wait_ge(oidx_ready, 2 * j + u + 1)
                    pool.sem_inc(pool_went_on, 1)
                    pool.indirect_dma_start(io["out"], bass.IndirectOffsetOnAxis(ap=oidx[u][:, 0:1], axis=0), og[u][:, :], None,
                                            bounds_check=N - 1, oob_is_err=False).then_inc(out_stored[u], 16)

            pipelined(pool, NT2 // 2, [(0, x_store)])
        @block.scalar
        def _(act):
            act.dma_start(ident[:, :], io["ident"]).then_inc(consts_in, 16)
            act.dma_start(nid[:, :], io["nid"]).then_inc(consts_in, 16)
            act.dma_start(eps_c[:, :], io["eps"]).then_inc(consts_in, 16)
            act.dma_start(ewf[:, :], io["ew"]).then_inc(consts_in, 16)
            act.dma_start(ewm[:, :], io["ewm"]).then_inc(consts_in, 16)
            act.dma_start(thr[:, :], io["thr"]).then_inc(consts_in, 16)
            act.dma_start(iota_i[:, :], io["iota_items"].partition_broadcast(64)).then_inc(consts_in, 16)
            act.dma_start(dlast_i[:, :], io["dst_last"]).then_inc(consts_in, 16)
            act.dma_start(src_t[:, :], io["src_t"]).then_inc(edges_in, 16)
            sq = r1[0:P, :].rearrange("p (t c) -> p t c", c=C)
            act.wait_ge(prep, 6)
            act.activation(sq, xt[:, :, :], ACT.Square).then_inc(sq_ready, 1)
            act.wait_ge(var_ready, 1)
            act.wait_ge(consts_in, 16 * 8)
            act.activation(xvar[:, :], xvar[:, :], ACT.Sqrt, bias=eps_c[0:P, :], scale=1.0 / C).then_inc(sd_ready, 1)

            def a_xT(i):
                for u in range(2):
                    act.wait_ge(xT_done, 2 * i + u + 1)
                    wait(act, mm_done, 2 * i + u - 1)
                    wait(act, xnT_copied, 2 * i + u - 1)
                    act.activation(xT[u][:, :, :], bank[u][:, 0:KC * P].rearrange("p (k n) -> p k n", k=KC), ACT.Copy).then_inc(xT_ready, 1)

            def a_exp(i):
                for u in range(2):
                    act.wait_ge(kv_added, 2 * i + u + 1)
                    wait(act, kphi_ready, 2 * i + u - 1)
                    act.activation(ek[u][:, :], kvb[u][:, 0:C], ACT.Exp).then_inc(k_exped, 1)

            def a_h(i):
                for u in range(2):
                    act.wait_ge(mm_done, 2 * i + u + 1)
                    wait(act, h_stored[u], 16 * i)
                    wait(act, split_step, 10 * i + 5 * u - 5)
                    act.activation(hs[u][:, :], bank[2 + u][0:P, 0:8 + C + 8], ACT.Copy).then_inc(hs_copied, 1)

            pipelined(act, SB, [(0, a_xT), (1, a_exp), (0, a_h)])

            act.wait_ge(kv_summed, 1)
            for u in range(2):
                act.wait_ge(h_stored[u], 16 * SB)
                act.wait_ge(hb_stored[u], 16 * SB)
            act.wait_ge(routed_filled, 16)
            act.wait_ge(items_ready, 1)
            act.dma_start(wq[:, :, :], io["wq"]).then_inc(wb_in, 16)
            act.dma_start(bq[:, :], io["bq"]).then_inc(wb_in, 16)
            act.dma_start(wo[:, :, :], io["wo"]).then_inc(wb_in, 16)
            act.dma_start(vec[:, :, :], io["vec"]).then_inc(wb_in, 16)
            act.dma_start(kvm[:, :], io["kvm"]).then_inc(wb_in, 16)
            act.dma_start(b1m[:, :], io["b1m"]).then_inc(wb_in, 16)
            act.wait_ge(wb_in, 96)

            def b_exp(i):
                act.wait_ge(q_ready, i + 1)
                wait(act, qphi_ready, i)
                for k in range(KC):
                    e = act.activation(eq[:, k, :], bank[0][:, k * W2T:(k + 1) * W2T], ACT.Exp, bias=bq[:, k:k + 1])
                e.then_inc(q_exped, 1)

            def b_atT(i):
                act.wait_ge(t_ready, i + 1)
                wait(act, o_ready, i)
                act.activation(atT[:, :, :, :].rearrange("p u k n -> p (u k n)"), bank[3][:, 0:4 * P], ACT.Copy).then_inc(atT_ready, 1)

            pipelined(act, SB, [(2, b_atT), (0, b_exp)])

            act.wait_ge(q_ready, SB)
            act.dma_start(w1m, io["w1m"]).then_inc(wf_in, 16)
            act.dma_start(w2m, io["w2m"]).then_inc(wf_in, 16)

            def f_sd1(i):
                for u in range(2):
                    act.wait_ge(ln1_var, 2 * i + u + 1)
                    act.activation(sd[u][:, 0, 0:1], mv[u][:, 0, 1:2], ACT.Sqrt, bias=eps_c[0:P, :]).then_inc(ln1_sd, 1)

            def f_ynT(i):
                act.wait_ge(yT_done, i + 1)
                wait(act, f_mm, JF * i)
                act.activation(ynT.rearrange("p k n -> p (k n)"), bank[0][:, 0:KC * W2T], ACT.Copy).then_inc(ynT_ready, 1)

            def f_sd2(i):
                for u in range(2):
                    act.wait_ge(ln2_var, 2 * i + u + 1)
                    act.activation(sd[u][:, 1, 0:1], mv[u][:, 1, 1:2], ACT.Sqrt, bias=eps_c[0:P, :]).then_inc(ln2_sd, 1)

            def f_relu_(i):
                wait(act, g_ready, i)
                for j in range(JF):
                    act.wait_ge(f_mm, JF * i + j + 1)
                    act.activation(f1[:, j, :], bank[1 + j % 2][:, 0:W2T], ACT.Relu, bias=b1m[:, j:j + 1]).then_inc(f_relu, 1)

            def f_load_x(i):
                wait(act, acc_ready, 2 * i)
                act.dma_start(xr[:, :, :], x_t[:, ds(2 * i, 2), :]).then_inc(xr_in, 16)

            def f_store(i):
                act.wait_ge(acc_ready, 2 * i + 2)
                act.dma_start(accd_t[:, ds(2 * i, 2), :], ac[:, :, :]).then_inc(acc_stored, 16)

            pipelined(act, SB, [(4, f_store), (3, f_load_x), (0, f_sd1), (3, f_sd2), (2, f_relu_), (1, f_ynT)])
            act.wait_ge(acc_stored, 16 * SB)

            act.wait_ge(attr_stored, 16 * len(COMBO))
            act.wait_ge(items_ready, 1)
            act.wait_ge(att_ones, IB)

            def load_item(j, b):
                s = item_reg(act, 0, IB * j + b)
                t = item_reg(act, 1, IB * j + b)
                act.dma_start(dstb[b][:, :], io["dst"][ds(s * SE, SE)].partition_broadcast(P)).then_inc(item_in[b], 16)
                act.dma_start(att[b][0:24, :], attrx[:, ds(s * SE, SE)]).then_inc(item_in[b], 16)
                act.dma_start(hbt[b][:, :, :].rearrange("p a c -> p (a c)"), hsplit[ds(t, 1)].rearrange("t p c -> p (t c)")).then_inc(item_in[b], 16)

            def e_relu(j, b, g):
                n = IB * j + b
                act.wait_ge(d_ready, 2 * n + g + 1)
                wait(act, prod_ready, 2 * n + g - 1)
                act.activation(enc[g][:, :, :].rearrange("p a c -> p (a c)"), bank[4 + g][:, :], ACT.Relu).then_inc(enc_ready, 1)

            for b in range(IB):
                load_item(0, b)

            def e_enc(j):
                for b in range(IB):
                    e_relu(j, b, 0)
                    e_relu(j, b, 1)
                    load_item(j + 1, b)

            pipelined(act, JI - 1, [(0, e_enc)])
            for b in range(IB):
                e_relu(JI - 1, b, 0)
                e_relu(JI - 1, b, 1)

            def s_copy(i):
                for u in range(2):
                    act.wait_ge(bt_ready, 2 * i + u + 1)
                    at0 = (2 * i + u) * 7 * 128
                    act.activation(bl[:, ds(at0, 512)], bank[2 * u][:, :], ACT.Copy)
                    act.activation(bl[:, ds(at0 + 512, 384)], bank[2 * u + 1][:, 0:384], ACT.Copy).then_inc(bl_copied, 1)

            with act.Fori(0, 7) as i:
                s_copy(i)
            def s_exp(i):
                for u in range(2):
                    act.wait_ge(dif_ready, 2 * i + u + 1)
                    act.activation(sst[u][:, :], sst[u][:, :], ACT.Exp).then_inc(exp_ready, 1)

            exb = ex.rearrange("p (c b h) -> p b c h", c=ROWS, b=BLK)

            def s_back(i):
                for u in range(2):
                    act.wait_ge(xt_ready, 2 * i + u + 1)
                    b0 = (2 * i + u) * 7
                    act.activation(exb[:, ds(b0, 4)], bank[2 * u][:, :].rearrange("p (b c h) -> p b c h", b=4, c=ROWS), ACT.Copy)
                    act.activation(exb[:, ds(b0 + 4, 3)], bank[2 * u + 1][:, 0:384].rearrange("p (b c h) -> p b c h", b=3, c=ROWS), ACT.Copy).then_inc(ex_copied, 1)

            with act.Fori(0, 7) as i:
                s_exp(i)
                s_back(i)
            act.wait_ge(ex_copied, 14)

            def m_den(j):
                for b in range(IB):
                    n = IB * j + b
                    s = item_reg(act, 0, n)
                    for g in range(2):
                        wait(act, m_used, 2 * n + g - 1)
                        act.activation(msg[g][:, :, C:HW], ex3[:, ds(4 * s + 2 * g, 2), :], ACT.Copy).then_inc(msgd_ready, 1)

            pipelined(act, JI, [(0, m_den)])
            act.wait_ge(x2_ready, T)
            act.activation(pack[:, :, 1], pack[:, :, 1], ACT.Sqrt, bias=eps_c[0:P, :]).then_inc(dsd_ready, 1)
            act.wait_ge(wr_in, 16 * 7)

            def d_xT(i):
                act.wait_ge(xdt_done, i + 1)
                wait(act, dh_mm, JF * i)
                act.activation(xdT[:, :, 0:W2T], bank[0][:, 0:KC * W2T].rearrange("p (k n) -> p k n", k=KC), ACT.Copy).then_inc(xdT_ready, 1)

            def d_gelu(i):
                wait(act, lg_mm, i)
                for j in range(JF):
                    act.wait_ge(dh_mm, JF * i + j + 1)
                    act.activation(hT[:, j, 0:W2T], bank[1 + j % 2][:, 0:W2T], ACT.Gelu, bias=b1f[:, j:j + 1]).then_inc(dh_gelu, 1)

            pipelined(act, SB, [(1, d_gelu), (0, d_xT)])
            act.wait_ge(r_step, 2)
            act.activation(rt[1][:, :], rt[0][:, :], ACT.Exp).then_inc(r_exp, 1)
            act.wait_ge(route_ready, 1)

            def d_rows(i):
                for u in range(2):
                    wait(act, scattered[u], 16 * i)
                    act.activation(srow[u][:, 0:C], x2[:, ds(2 * i + u, 1), :].rearrange("p t c -> p (t c)"), ACT.Copy).then_inc(srow_ready[u], 1)

            pipelined(act, SB, [(0, d_rows)])

            def x_T(i):
                act.wait_ge(gT_done, i + 1)
                wait(act, gh_mm, JF * i)
                act.activation(xdT.rearrange("p k n -> p (k n)"), bank[0][:, :], ACT.Copy).then_inc(gT_ready, 1)

            def x_gelu(i):
                for u in range(2):
                    wait(act, y_ready, 2 * i + u - 1)
                for j in range(JF):
                    act.wait_ge(gh_mm, JF * i + j + 1)
                    act.activation(hT[:, j, :], bank[1 + j % 2][:, 0:256], ACT.Gelu, bias=b1f[:, j:j + 1]).then_inc(gh_gelu, 1)

            pipelined(act, NT2 // 2, [(1, x_gelu), (0, x_T)])

        @block.tensor
        def _(pe):
            pe.wait_ge(wa_in, 16 * 5)
            for k in range(KC):
                for o in range(KC):
                    m = pe.matmul(bank[k][:, 0:16], wg[:, o, k * 128:(k + 1) * 128], abd[:, o, :], start=(o == 0), stop=(o == KC - 1))
            m.then_inc(setup_mm, 1)
            pe.wait_ge(prep, 5)
            pe.wait_ge(consts_in, 16 * 8)
            pe.matmul(bank[2][0:64, 0:NS], ones_s[:, :], dlast[:, :], start=True, stop=True).then_inc(setup_mm, 1)
            pe.wait_ge(setup_ev, 6)
            pe.matmul(bank[3][0:1, 0:ITP], thr[:, 2:3], lastb[:, :], start=True, stop=True).then_inc(setup_mm, 1)
            pe.wait_ge(setup_ev, 7)

            def a_T(i):
                for u in range(2):
                    pe.wait_ge(xs_ready, 2 * i + u + 1)
                    wait(pe, xT_ready, 2 * i + u - 1)
                    for k in range(KC):
                        m = pe.transpose(bank[u][:, k * P:(k + 1) * P], xs[u][:, k * 128:(k + 1) * 128], ident[0:P, 0:P])
                    m.then_inc(xT_done, 1)

            def a_mm(i):
                for u in range(2):
                    pe.wait_ge(xT_ready, 2 * i + u + 1)
                    wait(pe, hs_copied, 2 * i + u - 1)
                    wait(pe, kv_added, 2 * i + u - 1)
                    for k in range(KC):
                        pe.matmul(bank[2 + u][0:P, 0:8 + C + 8], xT[u][:, k, :], wh[:, k, :], start=(k == 0), stop=(k == KC - 1))
                    for k in range(KC):
                        m = pe.matmul(bank[4 + u][0:P, :], xT[u][:, k, :], wkv[:, k, :], start=(k == 0), stop=(k == KC - 1))
                    m.then_inc(mm_done, 1)

            def a_kv(i):
                for u in range(2):
                    pe.wait_ge(kphi_ready, 2 * i + u + 1)
                    for k in range(KC):
                        m = pe.matmul(bank[6 + k][:, 0:129], kphi[u][:, k * 128:(k + 1) * 128], kvb[u][:, C + 129 * k:C + 129 * (k + 1)],
                                      start=False, stop=False, skip_group_check=True)
                    m.then_inc(kv_acc, 1)

            pe.wait_ge(setup_ev, 7)
            for k in range(KC):
                pe.matmul(bank[6 + k][:, 0:129], zrow[:, 0:128], zrow[:, 0:129], start=True, stop=False, skip_group_check=True)
            pipelined(pe, SB, [(0, a_T), (0, a_mm), (1, a_kv)])
            for k in range(KC):
                m = pe.matmul(bank[6 + k][:, 0:129], zrow[:, 0:128], zrow[:, 0:129], start=False, stop=True, skip_group_check=True)
            m.then_inc(kv_summed, 1)

            pe.wait_ge(xnT_copied, 2 * SB)
            pe.wait_ge(wb_in, 96)
            pe.wait_ge(kvr_ready, 2 * KC)

            def b_q(i):
                wait(pe, qphi_ready, i)
                for o in range(KC):
                    for k in range(KC):
                        m = pe.matmul(bank[0][:, o * W2T:(o + 1) * W2T], wq[:, k, o * 128:(o + 1) * 128], xnT[:, k, ds(i * W2T, W2T)], start=(k == 0), stop=(k == KC - 1))
                m.then_inc(q_ready, 1)

            def b_num(i):
                pe.wait_ge(qphi_ready, i + 1)
                for u in range(2):
                    wait(pe, at_ready, 2 * i + u - 1)
                    for k in range(KC):
                        m = pe.matmul(bank[1 + u][0:P, 132 * k:132 * (k + 1)], qphi[:, k, u * P:(u + 1) * P], kvr[:, k, :], start=True, stop=True)
                m.then_inc(n_ready, 1)

            def b_T(i):
                wait(pe, atT_ready, i)
                for u in range(2):
                    pe.wait_ge(at_ready, 2 * i + u + 1)
                    for k in range(KC):
                        m = pe.transpose(bank[3][:, (2 * u + k) * P:(2 * u + k + 1) * P], at[u][:, k * 128:(k + 1) * 128], ident[0:P, 0:P])
                m.then_inc(t_ready, 1)

            def b_o(i):
                pe.wait_ge(atT_ready, i + 1)
                for u in range(2):
                    wait(pe, y1_read, 2 * i + u - 1)
                    for k in range(KC):
                        m = pe.matmul(bank[4 + u][0:P, 0:C], atT[:, u, k, :], wo[:, k, :], start=(k == 0), stop=(k == KC - 1))
                m.then_inc(o_ready, 1)

            pipelined(pe, SB, [(3, b_o), (2, b_T), (1, b_num), (0, b_q)])

            pe.wait_ge(wf_in, 32)
            pe.wait_ge(y1_read, 2 * SB)

            def f_T(i):
                wait(pe, ynT_ready, i)
                for u in range(2):
                    pe.wait_ge(yn_ready, 2 * i + u + 1)
                    for k in range(KC):
                        m = pe.transpose(bank[0][:, k * W2T + u * P:k * W2T + (u + 1) * P], yn[u][:, k * 128:(k + 1) * 128], ident[0:P, 0:P])
                m.then_inc(yT_done, 1)

            def f_ff(i):
                pe.wait_ge(ynT_ready, i + 1)
                for j in range(JF):
                    wait(pe, f_relu, JF * i + j - 1)
                    for k in range(KC):
                        m = pe.matmul(bank[1 + j % 2][:, 0:W2T], w1m[:, k, j * 128:(j + 1) * 128], ynT[:, k, :], start=(k == 0), stop=(k == KC - 1))
                    m.then_inc(f_mm, 1)
                for u in range(2):
                    wait(pe, z_read, 2 * i + u - 1)
                    for j in range(JF):
                        if u == 0:
                            pe.wait_ge(f_relu, JF * i + j + 1)
                        m = pe.matmul(bank[3 + u][0:P, 0:C], f1[:, j, u * P:(u + 1) * P], w2m[:, j, :], start=(j == 0), stop=(j == JF - 1))
                m.then_inc(g_ready, 1)

            pipelined(pe, SB, [(1, f_T), (2, f_ff)])

            pe.wait_ge(z_read, 2 * SB)

            def e_mm(j):
                for b in range(IB):
                    n = IB * j + b
                    pe.wait_ge(item_in[b], 48 * j + 48)
                    for g in range(2):
                        wait(pe, enc_ready, 2 * n + g - 1)
                        for c in range(2):
                            e0 = (2 * g + c) * 128
                            pe.matmul(bank[4 + g][:, c * C:(c + 1) * C], att[b][:, e0:e0 + 128], ew_bf[:, :], start=True, stop=True)
                        pe.wait_ge(oneh_t_ready, 2 * n + g + 1)
                        wait(pe, d_read, 2 * n + g - 1)
                        for c in range(2):
                            for a in range(3):
                                m = pe.matmul(bank[2 * g + c][:, 0:HW], oneh_t[g][:, c * 128:(c + 1) * 128], hbt[b][:, a, :], start=(a == 0), stop=(a == 2))
                        m.then_inc(d_ready, 1)

            pipelined(pe, JI, [(0, e_mm)])

            pe.wait_ge(d_read, 2 * ITEMS)

            def to_rows(ready, copied, done, i):
                for u in range(2):
                    pe.wait_ge(ready, 2 * i + u + 1)
                    wait(pe, copied, 2 * i + u - 1)
                    for b in range(7):
                        m = pe.transpose(bank[2 * u + b // 4][:, (b % 4) * 128:(b % 4 + 1) * 128], sst[u][:, b * 128:(b + 1) * 128], ident[:, :])
                    m.then_inc(done, 1)

            pipelined(pe, 7, [(0, lambda i: to_rows(sst_ready, bl_copied, bt_ready, i))])
            pe.wait_ge(s_tr, 4)
            for n in range(4):
                m = pe.transpose(bank[4][0:1, n * 128:(n + 1) * 128], edge_v[:, n:n + 1], ident[:, :])
            m.then_inc(s_trc, 1)
            pe.wait_ge(s_tr, 6)
            for n in range(2):
                m = pe.transpose(bank[5][:, n:n + 1], rows[0:1, 10 + n, :], ident[0:1, 0:1])
            m.then_inc(s_trc, 1)
            pipelined(pe, 7, [(0, lambda i: to_rows(exp_ready, ex_copied, xt_ready, i))])

            pe.wait_ge(ex_copied, 14)

            def m_sum(j):
                for b in range(IB):
                    n = IB * j + b
                    wait(pe, acc_added, n - 1)
                    for g in range(2):
                        pe.wait_ge(msg_ready, 2 * n + g + 1)
                        pe.wait_ge(msgd_ready, 2 * n + g + 1)
                        for c in range(2):
                            m = pe.matmul(bank[b % 2][0:P, 0:HW], oneh[g][:, c, :], msg[g][:, c, :], start=(g + c == 0), stop=(g + c == 2))
                        m.then_inc(m_used, 1)

            m_sum(0)
            with pe.Fori(1, JI) as j:
                m_sum(j)

            pe.wait_ge(wr_in, 16 * 7)
            pe.wait_ge(acc_added, ITEMS)

            def d_T(i):
                wait(pe, xdT_ready, i)
                for u in range(2):
                    pe.wait_ge(xd_ready, 2 * i + u + 1)
                    for k in range(KC):
                        m = pe.transpose(bank[0][:, k * W2T + u * P:k * W2T + (u + 1) * P], xd[u][:, k * 128:(k + 1) * 128], ident[0:P, 0:P])
                m.then_inc(xdt_done, 1)

            def d_ff(i):
                pe.wait_ge(xdT_ready, i + 1)
                for j in range(JF):
                    wait(pe, dh_gelu, JF * i + j - 1)
                    for k in range(KC):
                        m = pe.matmul(bank[1 + j % 2][:, 0:W2T], w1f[:, k, j * 128:(j + 1) * 128], xdT[:, k, 0:W2T], start=(k == 0), stop=(k == KC - 1))
                    m.then_inc(dh_mm, 1)
                wait(pe, lg_ready, i)
                for u in range(2):
                    for j in range(JF):
                        if u == 0:
                            pe.wait_ge(dh_gelu, JF * i + j + 1)
                        m = pe.matmul(bank[3][0:P, u * NE:(u + 1) * NE], hT[:, j, u * P:(u + 1) * P], wgt[:, j, :], start=(j == 0), stop=(j == JF - 1))
                m.then_inc(lg_mm, 1)

            pipelined(pe, SB, [(0, d_T), (1, d_ff)])
            pe.wait_ge(r_step, 8)
            pe.matmul(bank[4][0:P, 0:T * NE], routec[0:P, 0:P], rt[2][:, :], start=True, stop=True)
            pe.matmul(bank[5][0:P, 0:T * NE], routec[0:P, P:2 * P], rt[2][:, :], start=True, stop=True).then_inc(r_mm, 1)

            pe.wait_ge(wd_in, 16)

            def x_T(i):
                wait(pe, gT_ready, i)
                for u in range(2):
                    pe.wait_ge(xgn_ready, 2 * i + u + 1)
                    for k in range(KC):
                        m = pe.transpose(bank[0][:, k * 256 + u * 128:k * 256 + (u + 1) * 128], xgn[u][:, k * 128:(k + 1) * 128], ident[:, :])
                m.then_inc(gT_done, 1)

            def x_ff(i):
                pe.wait_ge(gT_ready, i + 1)
                for j in range(JF):
                    wait(pe, gh_gelu, JF * i + j - 1)
                    for k in range(KC):
                        m = pe.matmul(bank[1 + j % 2][:, 0:256], w1f[:, k, j * 128:(j + 1) * 128], xdT[:, k, :], start=(k == 0), stop=(k == KC - 1))
                    m.then_inc(gh_mm, 1)
                for u in range(2):
                    e = pe.value_load(e_row[0:1, ds(2 * i + u, 1)], min_val=0, max_val=NE - 1)
                    wait(pe, og_ready, 2 * i + u - 1)
                    for j in range(JF):
                        if u == 0:
                            pe.wait_ge(gh_gelu, JF * i + j + 1)
                        pe.matmul(bank[3 + u][:, 0:C], hT[:, j, u * 128:(u + 1) * 128], wd[:, ds(e, 1), j * C:(j + 1) * C].rearrange("p e c -> p (e c)"), start=(j == 0), stop=False)
                    pe.matmul(bank[3 + u][:, 0:C], ones_r, bdr[:, ds(e * C, C)], start=False, stop=True).then_inc(y_ready, 1)

            pipelined(pe, NT2 // 2, [(1, x_ff), (0, x_T)])

        @block.vector
        def _(v):
            def own(value):
                v.wait_ge(own_step, value)

            v.wait_ge(edges_in, 32)
            for n in range(3):
                v.tensor_copy(attr_b[n], attr_f).then_inc(prep if n == 2 else own_step, 3 if n == 2 else 1)
                if n < 2:
                    own(2 * n + 1)
                    v.tensor_tensor(attr_f, attr_f, attr_b[n], ALU.subtract).then_inc(own_step, 1)
                    own(2 * n + 2)
            v.wait_ge(consts_in, 16 * 8)
            v.memset(ones_s[:, :], 1.0).then_inc(prep, 1)
            v.tensor_copy(dlast[:, :], dlast_i[:, :]).then_inc(prep, 1)
            v.tensor_copy(ewr[:, :], ewf[:, :]).then_inc(own_step, 1)
            own(5)
            for n in range(3):
                v.tensor_copy(ewp[:, n, :], ewr[:, :]).then_inc(own_step, 1)
                own(6 + 2 * n)
                v.tensor_tensor(ewr[:, :], ewr[:, :], ewp[:, n, :], ALU.subtract).then_inc(own_step, 1)
                own(7 + 2 * n)
            v.tensor_scalar(ewr[:, :], ewp[:, 0, :], ewm[:, 0:1], None, ALU.mult).then_inc(own_step, 1)
            own(12)
            v.scalar_tensor_tensor(ewr[:, :], ewp[:, 1, :], ewm[:, 1:2], ewr[:, :], ALU.mult, ALU.add).then_inc(own_step, 1)
            own(13)
            v.scalar_tensor_tensor(ew_bf[:, :], ewp[:, 2, :], ewm[:, 2:3], ewr[:, :], ALU.mult, ALU.add).then_inc(own_step, 1)
            v.wait_ge(x_in, 16)
            v.tensor_reduce(xsum[:, :], xt[:, :, :], X, ALU.add).then_inc(own_step, 1)
            own(15)
            v.tensor_scalar(xsum[:, :], xsum[:, :], 1.0 / C, None, ALU.mult).then_inc(own_step, 1)
            own(16)
            v.tensor_tensor(xt[:, :, :], xt[:, :, :], xsum[:, :].unsqueeze(2).to_broadcast([P, T, C]), ALU.subtract).then_inc(prep, 1)
            v.wait_ge(setup_mm, 1)
            for k in range(KC):
                v.tensor_copy(wh[:, k, 0:8], bank[k][:, 0:8]).then_inc(setup_ev, 1)
                v.tensor_copy(wh[:, k, 8 + C:], bank[k][:, 8:16]).then_inc(setup_ev, 1)
            v.wait_ge(setup_mm, 2)
            v.tensor_scalar(lastb[:, 0:NS], bank[2][0:64, 0:NS], thr[:, 0:1], None, ALU.is_lt).then_inc(own_step, 1)
            own(17)
            v.tensor_reduce(cnt[:, 0:1], lastb[:, 0:NS], X, ALU.add).then_inc(own_step, 1)
            own(18)
            v.tensor_tensor(cnt[:, 1:2], cnt[:, 0:1], thr[:, 1:2], ALU.add).then_inc(setup_ev, 1)
            v.wait_ge(setup_ev, 5)
            v.tensor_scalar(lastb[:, :], iota_i[:, :], cnt[:, 1:2], None, ALU.is_ge).then_inc(setup_ev, 1)
            v.wait_ge(setup_mm, 3)
            v.tensor_copy(itf[:, ITP:], bank[3][0:1, 0:ITP]).then_inc(own_step, 1)
            own(19)
            v.tensor_tensor(itf[:, 0:ITP], iota_i[0:1, :], itf[:, ITP:], ALU.subtract).then_inc(own_step, 1)
            own(20)
            v.tensor_scalar(itf[:, 0:ITP], itf[:, 0:ITP], float(NS - 1), None, ALU.min).then_inc(own_step, 1)
            own(21)
            v.tensor_copy(items[:, :], itf[:, :]).then_inc(items_ready, 1)
            v.memset(zrow[:, :], 0.0).then_inc(setup_ev, 1)
            for u in range(2):
                v.memset(kvb[u][:, C:], 1.0).then_inc(setup_ev, 1)
            v.wait_ge(sq_ready, 1)
            v.tensor_reduce(xvar[:, :], r1[0:P, :].rearrange("p (t c) -> p t c", c=C), X, ALU.add).then_inc(var_ready, 1)
            v.wait_ge(sd_ready, 1)
            v.reciprocal(xvar[:, :], xvar[:, :]).then_inc(own_step, 1)
            own(22)
            v.tensor_tensor(xt[:, :, :], xt[:, :, :], xvar[:, :].unsqueeze(2).to_broadcast([P, T, C]), ALU.mult).then_inc(own_step, 1)
            own(23)
            v.wait_ge(setup_ev, 9)

            def a_xs(i):
                for u in range(2):
                    wait(v, xT_done, 2 * i + u - 1)
                    v.tensor_copy(xs[u][:, :], xt[:, ds(2 * i + u, 1), :].rearrange("p t c -> p (t c)")).then_inc(xs_ready, 1)

            def a_phi(i):
                for u in range(2):
                    v.wait_ge(k_exped, 2 * i + u + 1)
                    wait(v, kv_acc, 2 * i + u - 1)
                    v.tensor_scalar(ek[u][:, :], ek[u][:, :], 1.0, None, ALU.min).then_inc(k_pos, 1)
                    v.wait_ge(k_pos, 2 * i + u + 1)
                    v.scalar_tensor_tensor(kphi[u][:, :], kvb[u][:, 0:C], 0.0, ek[u][:, :], ALU.max, ALU.add).then_inc(kphi_ready, 1)

            def a_kv(i):
                for u in range(2):
                    v.wait_ge(mm_done, 2 * i + u + 1)
                    wait(v, kv_acc, 2 * i + u - 1)
                    wait(v, kphi_ready, 2 * i + u - 1)
                    v.tensor_tensor(kvb[u][:, 0:C], bank[4 + u][0:P, 0:C], bkv[:, 0:C], ALU.add)
                    v.tensor_tensor(kvb[u][:, C:].rearrange("p (k c) -> p k c", k=KC)[:, :, 0:128], bank[4 + u][0:P, C:].rearrange("p (k c) -> p k c", k=KC),
                                    bkv[:, C:].rearrange("p (k c) -> p k c", k=KC), ALU.add).then_inc(kv_added, 1)

            pipelined(v, SB, [(0, a_xs), (1, a_phi), (0, a_kv)])

            v.wait_ge(kv_summed, 1)
            v.wait_ge(wb_in, 96)
            for k in range(KC):
                v.tensor_tensor(kvr[:, k, 0:128], bank[6 + k][:, 0:128], kvm[:, 0:128], ALU.mult).then_inc(kvr_ready, 1)
                v.tensor_scalar(kvr[:, k, 128:132], kvm[:, 128:132], bank[6 + k][:, 128:129], None, ALU.mult).then_inc(kvr_ready, 1)
            v.tensor_tensor(vec[:, 5, :], vec[:, 5, :], vec[:, 6, :], ALU.add).then_inc(own_step, 1)
            own(24)

            def b_phi(i):
                v.wait_ge(q_exped, i + 1)
                wait(v, qphi_ready, i)
                for k in range(KC):
                    m = v.tensor_scalar(rq[:, k, :], bank[0][:, k * W2T:(k + 1) * W2T], bq[:, k:k + 1], 0.0, ALU.add, ALU.max)
                m.then_inc(q_relu, 1)
                v.wait_ge(q_relu, i + 1)
                wait(v, n_ready, i)
                v.scalar_tensor_tensor(qphi[:, :, :].rearrange("p k n -> p (k n)"), eq[:, :, :].rearrange("p k n -> p (k n)"), 1.0,
                                       rq[:, :, :].rearrange("p k n -> p (k n)"), ALU.min, ALU.add).then_inc(qphi_ready, 1)

            def b_at(i):
                v.wait_ge(n_ready, i + 1)
                wait(v, t_ready, i)
                num = [bank[1 + u][0:P, 0:264].rearrange("p (k c) -> p k c", k=KC) for u in range(2)]
                for u in range(2):
                    wait(v, at_ready, 2 * i + u - 1)
                    v.tensor_scalar(den[u][:, 0, :].rearrange("p (k g) -> p k g", k=KC), num[u][:, :, 128:132], 1e-6, None, ALU.add).then_inc(den_step[u], 1)
                for u in range(2):
                    v.wait_ge(den_step[u], 2 * i + 1)
                    v.reciprocal(den[u][:, 1, :], den[u][:, 0, :]).then_inc(den_step[u], 1)
                for u in range(2):
                    v.wait_ge(den_step[u], 2 * i + 2)
                    v.tensor_tensor(at[u][:, :].rearrange("p (k g d) -> p k g d", k=KC, d=D), num[u][:, :, 0:128].rearrange("p k (g d) -> p k g d", d=D),
                                    den[u][:, 1, :].rearrange("p (k g) -> p k g", k=KC).unsqueeze(3).to_broadcast([P, KC, 4, D]), ALU.mult).then_inc(at_ready, 1)

            def b_y(i):
                v.wait_ge(o_ready, i + 1)
                wait(v, y1_ready, 2 * i)
                for u in range(2):
                    v.tensor_tensor(y1t[u][:, :], bank[4 + u][0:P, 0:C], vec[0:P, 0, :], ALU.add).then_inc(y1_read, 1)
                for u in range(2):
                    v.wait_ge(y1_read, 2 * i + u + 1)
                    xv = xt[:, ds(2 * i + u, 1), :].rearrange("p t c -> p (t c)")
                    v.tensor_tensor(xv, xv, y1t[u][:, :], ALU.add).then_inc(y1_ready, 1)

            pipelined(v, SB, [(3, b_y), (1, b_at), (0, b_phi)])

            v.wait_ge(y1_ready, T)

            def f_stats(i):
                for u in range(2):
                    xv = xt[:, ds(2 * i + u, 1), :].rearrange("p t c -> p (t c)")
                    v.bn_stats(st[u][:, 0, :], xv).then_inc(st_ready, 1)
                for u in range(2):
                    v.wait_ge(st_ready, 2 * i + u + 1)
                    wait(v, ln1_sd, 2 * i + u - 1)
                    wait(v, ln_step[u], 4 * i - 2)
                    v.sem_inc(vec_went_on, 1)
                    v.bn_aggr(mv[u][:, 0, :], st[u][:, 0, :]).then_inc(ln1_var, 1)

            def f_norm(i):
                xv = [xt[:, ds(2 * i + u, 1), :].rearrange("p t c -> p (t c)") for u in range(2)]
                for u in range(2):
                    v.wait_ge(ln1_sd, 2 * i + u + 1)
                    v.reciprocal(sd[u][:, 0, 1:2], sd[u][:, 0, 0:1]).then_inc(ln_step[u], 1)
                for u in range(2):
                    v.wait_ge(ln_step[u], 4 * i + 1)
                    v.tensor_scalar(xv[u], xv[u], mv[u][:, 0, 0:1], sd[u][:, 0, 1:2], ALU.subtract, ALU.mult).then_inc(ln_step[u], 1)
                for u in range(2):
                    v.wait_ge(ln_step[u], 4 * i + 2)
                    v.tensor_tensor(xv[u], xv[u], vec[0:P, 2, :], ALU.mult).then_inc(ln_step[u], 1)
                for u in range(2):
                    v.wait_ge(ln_step[u], 4 * i + 3)
                    v.tensor_tensor(xv[u], xv[u], vec[0:P, 3, :], ALU.add).then_inc(ln_step[u], 1)
                for u in range(2):
                    v.wait_ge(ln_step[u], 4 * i + 4)
                    wait(v, yT_done, i)
                    v.tensor_scalar(yn[u][:, :], xv[u], 1.0, None, ALU.mult).then_inc(yn_ready, 1)

            def f_res(i):
                v.wait_ge(g_ready, i + 1)
                for u in range(2):
                    xv = xt[:, ds(2 * i + u, 1), :].rearrange("p t c -> p (t c)")
                    wait(v, acc_ready, 2 * i + u - 1)
                    v.tensor_tensor(y2[u][:, :], bank[3 + u][0:P, 0:C], xv, ALU.add).then_inc(z_read, 1)
                for u in range(2):
                    v.wait_ge(z_read, 2 * i + u + 1)
                    v.tensor_tensor(y2[u][:, :], y2[u][:, :], vec[0:P, 1, :], ALU.add).then_inc(st2_ready[u], 1)
                for u in range(2):
                    v.wait_ge(st2_ready[u], 2 * i + 1)
                    v.bn_stats(st[u][:, 1, :], y2[u][:, :]).then_inc(st2_ready[u], 1)
                for u in range(2):
                    v.wait_ge(st2_ready[u], 2 * i + 2)
                    v.sem_inc(vec_went_on, 1)
                    v.bn_aggr(mv[u][:, 1, :], st[u][:, 1, :]).then_inc(ln2_var, 1)

            def f_out(i):
                for u in range(2):
                    v.wait_ge(ln2_sd, 2 * i + u + 1)
                    v.reciprocal(sd[u][:, 1, 1:2], sd[u][:, 1, 0:1]).then_inc(ln2_step[u], 1)
                for u in range(2):
                    v.wait_ge(ln2_step[u], 4 * i + 1)
                    v.tensor_scalar(y2[u][:, :], y2[u][:, :], mv[u][:, 1, 0:1], sd[u][:, 1, 1:2], ALU.subtract, ALU.mult).then_inc(ln2_step[u], 1)
                for u in range(2):
                    v.wait_ge(ln2_step[u], 4 * i + 2)
                    v.tensor_tensor(y2[u][:, :], y2[u][:, :], vec[0:P, 4, :], ALU.mult).then_inc(ln2_step[u], 1)
                for u in range(2):
                    v.wait_ge(ln2_step[u], 4 * i + 3)
                    v.tensor_tensor(y2[u][:, :], y2[u][:, :], vec[0:P, 5, :], ALU.add).then_inc(ln2_step[u], 1)
                v.wait_ge(xr_in, 16 * i + 16)
                wait(v, acc_stored, 16 * i)
                for u in range(2):
                    v.wait_ge(ln2_step[u], 4 * i + 4)
                    v.tensor_tensor(ac[:, u, :], y2[u][:, :], xr[:, u, :], ALU.add).then_inc(acc_ready, 1)

            pipelined(v, SB, [(1, f_norm), (0, f_stats), (3, f_out), (2, f_res)])

            v.wait_ge(acc_stored, 16 * SB)
            for b in range(IB):
                v.memset(att[b][:, :], 1.0).then_inc(att_ones, 1)
            v.memset(ad, 0.0).then_inc(ad_zero, 1)
            v.wait_ge(items_ready, 1)

            def e_onehot(j, b, g, t):
                n = IB * j + b
                if g == 0:
                    v.wait_ge(item_in[b], 48 * j + 48)
                wait(v, d_ready, 2 * n + g - 1)
                v.tensor_scalar(oneh_t[g][:, :], dstb[b][:, g * 256:(g + 1) * 256], nid[0:P, ds(t, 1)], None, ALU.is_equal).then_inc(oneh_t_ready, 1)

            def e_reduce(j, b, g, s):
                n = IB * j + b
                v.wait_ge(enc_ready, 2 * n + g + 1)
                pd = [bank[2 * g + c] for c in range(2)]
                wait(v, red_ready, 2 * n + g - 1)
                for c in range(2):
                    m = v.tensor_tensor(prod[g][:, c, :], pd[c][:, 0:C], enc[g][:, c, :], ALU.mult)
                m.then_inc(prod_ready, 1)
                v.wait_ge(prod_ready, 2 * n + g + 1)
                v.tensor_reduce(red[g][:, :, :], prod[g][:, :, :].rearrange("p c (h d) -> p c h d", d=D), X, ALU.add).then_inc(red_ready, 1)
                v.wait_ge(red_ready, 2 * n + g + 1)
                wait(v, ad_added, 2 * n + g - 1)
                for c in range(2):
                    m = v.tensor_tensor(red2[g][:, c, :], pd[c][:, C:HW], red[g][:, c, :], ALU.add)
                m.then_inc(d_read, 1)
                v.wait_ge(d_read, 2 * n + g + 1)
                wait(v, ad_added, 2 * n + g)
                a = ad3[:, ds(4 * s + 2 * g, 2), :]
                v.tensor_tensor(a, a, red2[g][:, :, :], ALU.add).then_inc(ad_added, 1)

            v.wait_ge(ad_zero, 1)

            def e_step(j):
                for b in range(IB):
                    t = item_reg(v, 1, IB * j + b)
                    for g in range(2):
                        e_onehot(j, b, g, t)
                        if (b, g) != (0, 0):
                            pb = b if g else b - 1
                            e_reduce(j, pb, 1 - g, item_reg(v, 0, IB * j + pb))
                        elif not isinstance(j, int):
                            e_reduce(j - 1, IB - 1, 1, item_reg(v, 0, IB * j - 1))

            e_step(0)
            with v.Fori(1, JI) as j:
                e_step(j)
            e_reduce(JI - 1, IB - 1, 1, item_reg(v, 0, ITEMS - 1))

            v.wait_ge(asrc_kept, NS)
            for b in range(GB):
                v.wait_ge(spilled[b], 16 * (NS // GB))
            v.wait_ge(ad_added, 2 * ITEMS)
            alb = al[:, :].rearrange("p (c b h) -> p b c h", c=ROWS, b=BLK)
            adb = ad.rearrange("p (c b h) -> p b c h", c=ROWS, b=BLK)

            def s_add(i):
                for u in range(2):
                    wait(v, bt_ready, 2 * i + u - 1)
                    b0 = (2 * i + u) * 7
                    v.tensor_tensor(sst[u][:, :].rearrange("p (b c h) -> p b c h", b=7, c=ROWS), alb[:, ds(b0, 7)], adb[:, ds(b0, 7)], ALU.add).then_inc(sst_ready, 1)

            pipelined(v, 7, [(0, s_add)])
            k = [0]

            def link(m):
                k[0] += 1
                m.then_inc(s_step, 1)
                v.wait_ge(s_step, k[0])

            v.wait_ge(dst_row_in, 16 * H)
            link(v.tensor_tensor(flag[:, 1:RL], dbi[:, 1:RL], dbi[:, 0:RL - 1], ALU.is_equal))
            v.tensor_copy(edge_v[:, 2:3], dbi[:, 0:1]).then_inc(s_tr, 1)
            v.tensor_copy(edge_v[:, 3:4], dbi[:, RL - 1:RL]).then_inc(s_tr, 1)
            v.wait_ge(s_tr, 2)
            link(v.tensor_scalar(flag[:, 1:RL], flag[:, 1:RL], BIG, -BIG, ALU.mult, ALU.add))
            link(v.memset(flag[:, 0:1], 0.0))
            link(v.memset(flag[:, RL:RL + 1], 0.0))
            v.wait_ge(bl_copied, 14)
            link(v.scalar_tensor_tensor(bl[:, :], bl[:, :], 0.2, bl[:, :], ALU.mult, ALU.max))
            link(v.tensor_tensor_scan(run, flag[:, 0:RL], bl[:, :], -BIG, ALU.add, ALU.max))
            v.tensor_copy(edge_v[:, 0:1], run[:, RL - 1:RL]).then_inc(s_tr, 1)
            v.wait_ge(s_tr, 3)
            link(v.tensor_tensor_scan(run[:, ::-1], flag[:, 1:RL + 1][:, ::-1], bl[:, ::-1], -BIG, ALU.add, ALU.max))
            v.tensor_copy(edge_v[:, 1:2], run[:, 0:1]).then_inc(s_tr, 1)
            v.wait_ge(s_trc, 1)
            for n in range(4):
                link(v.tensor_copy(rows[:, n, :].rearrange("o (h c) -> o h c", h=H), bank[4][0:1, n * 128:(n + 1) * 128].rearrange("o (c h) -> o h c", h=H)))
            last_f, first_b, first_d, last_d = (rows[:, n, :].rearrange("o (h c) -> o h c", h=H) for n in range(4))
            same, whole, pen_f, pen_b, car, tot = (rows[:, 4 + n, :].rearrange("o (h c) -> o h c", h=H) for n in range(6))
            R = ROWS
            link(v.memset(rows[:, 4:6, :], 0.0))
            link(v.tensor_tensor(same[:, :, 1:R], first_d[:, :, 1:R], last_d[:, :, 0:R - 1], ALU.is_equal))
            link(v.tensor_tensor(whole, first_d, last_d, ALU.is_equal))
            link(v.memset(rows[:, 6:8, :], 0.0))
            link(v.tensor_tensor(pen_f, same, whole, ALU.mult))
            link(v.tensor_tensor(pen_b[:, :, 0:R - 1], same[:, :, 1:R], whole[:, :, 0:R - 1], ALU.mult))
            link(v.tensor_scalar(rows[:, 6:8, :], rows[:, 6:8, :], BIG, -BIG, ALU.mult, ALU.add))
            link(v.tensor_tensor_scan(rows[:, 9, :], rows[:, 6, :], rows[:, 0, :], -BIG, ALU.add, ALU.max))
            link(v.tensor_scalar(rows[:, 8, :], rows[:, 4, :], BIG, -BIG, ALU.mult, ALU.add))
            link(v.tensor_tensor(rows[:, 10, :].rearrange("o (h c) -> o h c", h=H)[:, :, 1:R], tot[:, :, 0:R - 1], same[:, :, 1:R], ALU.mult))
            link(v.memset(rows[:, 10, :].rearrange("o (h c) -> o h c", h=H)[:, :, 0:1], 0.0))
            link(v.tensor_tensor(rows[:, 10, :], rows[:, 10, :], rows[:, 8, :], ALU.add))
            link(v.tensor_tensor_scan(rows[:, 9, ::-1], rows[:, 7, ::-1], rows[:, 1, ::-1], -BIG, ALU.add, ALU.max))
            bwd = rows[:, 11, :].rearrange("o (h c) -> o h c", h=H)
            link(v.memset(rows[:, 11, :], -BIG))
            link(v.tensor_tensor(bwd[:, :, 0:R - 1], tot[:, :, 1:R], same[:, :, 1:R], ALU.mult))
            link(v.tensor_tensor(bwd[:, :, 0:R - 1], bwd[:, :, 0:R - 1], car[:, :, 1:R], ALU.add))
            for n in range(2):
                link(v.tensor_copy(rows[:, n, :].rearrange("o (c h) -> o c h", h=H), rows[:, 10 + n, :].rearrange("o (h c) -> o c h", h=H)))
            for n in range(2):
                v.tensor_copy(rows[:, 10 + n, :], rows[:, n, :]).then_inc(s_tr, 1)
            v.wait_ge(s_trc, 2)
            link(v.tensor_copy(carry[:, :], bank[5][:, 0:2]))
            link(v.tensor_tensor_scan(run, flag[:, 0:RL], bl[:, :], carry[:, 0:1], ALU.add, ALU.max))
            link(v.tensor_tensor_scan(flag[:, 1:RL + 1][:, ::-1], flag[:, 1:RL + 1][:, ::-1], bl[:, ::-1], carry[:, 1:2], ALU.add, ALU.max))
            link(v.tensor_tensor(run, run, flag[:, 1:RL + 1], ALU.max))

            def s_dif(i):
                for u in range(2):
                    wait(v, xt_ready, 2 * i + u - 1)
                    c0 = ds((2 * i + u) * 7 * 128, 7 * 128)
                    v.tensor_tensor(sst[u][:, :], bl[:, c0], run[:, c0], ALU.subtract).then_inc(dif_ready, 1)

            pipelined(v, 7, [(0, s_dif)])

            v.wait_ge(nidx_in, 32)
            v.wait_ge(ex_copied, 14)
            v.tensor_copy(dst_f[:, :], dst_i[:, :]).then_inc(dstf_ready, 1)
            v.wait_ge(dstf_ready, 1)
            v.wait_ge(acc_zero, 1)

            def m_msg(j, b):
                n = IB * j + b
                s = item_reg(v, 0, n)
                t = item_reg(v, 1, n)
                v.wait_ge(hs_in[b], 16 * j + 16)
                for g in range(2):
                    wait(v, m_used, 2 * n + g - 1)
                    v.tensor_tensor(oneh[g][:, :, :], dst_f[:, ds(4 * s + 2 * g, 2)].unsqueeze(2).to_broadcast([128, 2, P]),
                                    nidx[:, ds(t * P, P)].unsqueeze(1).to_broadcast([128, 2, P]), ALU.is_equal)
                    v.tensor_tensor(msg[g][:, :, 0:C].rearrange("p c (h d) -> p c h d", d=D), hsb[b][:, g * 2 * C:(g + 1) * 2 * C].rearrange("p (c h d) -> p c h d", c=2, d=D),
                                    ex3[:, ds(4 * s + 2 * g, 2), :].unsqueeze(3).to_broadcast([128, 2, H, D]), ALU.mult).then_inc(msg_ready, 1)

            def m_acc(j, b):
                n = IB * j + b
                t = item_reg(v, 1, n)
                v.wait_ge(m_used, 2 * n + 2)
                wait(v, acc_added, n)
                a = acc[:, ds(t, 1), :].rearrange("p t c -> p (t c)")
                v.tensor_tensor(a, a, bank[b % 2][0:P, 0:HW], ALU.add).then_inc(acc_added, 1)

            def m_step(j):
                for b in range(IB):
                    m_msg(j, b)
                    if b:
                        m_acc(j, b - 1)
                    elif not isinstance(j, int):
                        m_acc(j - 1, IB - 1)

            m_step(0)
            with v.Fori(1, JI) as j:
                m_step(j)
            m_acc(JI - 1, IB - 1)
            v.wait_ge(acc_added, ITEMS)

            with v.Fori(0, SB) as i:
                v.wait_ge(xa_in, 16 * i + 16)
                tt = [acc[:, ds(2 * i + u, 1), :].rearrange("p t c -> p (t c)") for u in range(2)]
                xv = [x2[:, ds(2 * i + u, 1), :].rearrange("p t c -> p (t c)") for u in range(2)]
                for u in range(2):
                    v.tensor_scalar(dn[u][:, 0, :], tt[u][:, C:HW], 1e-10, None, ALU.max).then_inc(x2_step[u], 1)
                for u in range(2):
                    v.wait_ge(x2_step[u], 5 * i + 1)
                    v.reciprocal(dn[u][:, 1, :], dn[u][:, 0, :]).then_inc(x2_step[u], 1)
                for u in range(2):
                    v.wait_ge(x2_step[u], 5 * i + 2)
                    v.tensor_tensor(ag[u][:, :].rearrange("p (h d) -> p h d", d=D), tt[u][:, 0:C].rearrange("p (h d) -> p h d", d=D),
                                    dn[u][:, 1, :].unsqueeze(2).to_broadcast([P, H, D]), ALU.mult).then_inc(x2_step[u], 1)
                for u in range(2):
                    v.wait_ge(x2_step[u], 5 * i + 3)
                    v.tensor_tensor(xv[u], ag[u][:, :], xa[:, u, :], ALU.add).then_inc(x2_step[u], 1)
                for u in range(2):
                    v.wait_ge(x2_step[u], 5 * i + 4)
                    v.sem_inc(vec_went_on, 1)
                    v.bn_stats(dst_6[u][:, :], xv[u]).then_inc(x2_step[u], 1)
                for u in range(2):
                    v.wait_ge(x2_step[u], 5 * i + 5)
                    v.sem_inc(vec_went_on, 1)
                    v.bn_aggr(dmv[u][:, :], dst_6[u][:, :]).then_inc(x2_aggr, 1)
                for u in range(2):
                    v.wait_ge(x2_aggr, 2 * i + u + 1)
                    v.tensor_scalar(pack[:, ds(2 * i + u, 1), 0:2].rearrange("p t c -> p (t c)"), dmv[u][:, :], 1.0, None, ALU.mult).then_inc(x2_ready, 1)
            v.wait_ge(dsd_ready, 1)
            v.reciprocal(pack[:, :, 1], pack[:, :, 1]).then_inc(drs_ready, 1)
            v.wait_ge(drs_ready, 1)
            v.wait_ge(wr_in, 16 * 7)

            def d_xn(i):
                wait(v, xdt_done, i)
                for u in range(2):
                    t = ds(2 * i + u, 1)
                    v.tensor_scalar(xd[u][:, :], x2[:, t, :].rearrange("p t c -> p (t c)"), pack[:, t, 0], pack[:, t, 1], ALU.subtract, ALU.mult).then_inc(xd_ready, 1)

            def d_lg(i):
                v.wait_ge(lg_mm, i + 1)
                for u in range(2):
                    m = v.tensor_tensor(lg[:, ds(2 * i + u, 1), :].rearrange("p t e -> p (t e)"), bank[3][0:P, u * NE:(u + 1) * NE], bg[:, :], ALU.add)
                m.then_inc(lg_ready, 1)

            pipelined(v, SB, [(0, d_xn), (2, d_lg)])
            v.wait_ge(lg_ready, SB)
            k = [0]

            def step(m):
                k[0] += 1
                m.then_inc(r_step, 1)
                v.wait_ge(r_step, k[0])

            o = 2 * P
            reset, wts, jrow = routec[0:P, o:o + 400], routec[0:P, o + 400:o + 408], routec[0:1, o + 408:o + 472]
            tok = routec[0:P, o + 473:o + 523]

            def te(a):
                return a.rearrange("p (t e) -> p t e", e=NE)

            mx, fw, sm, pos = rs[0][:, 0:T], rs[1][:, 0:T], rs[2][:, 0:T], rs[3][:, 0:T]
            step(v.tensor_reduce(mx, lg[:, :, :], X, ALU.max))
            step(v.tensor_tensor(te(rt[0][:, :]), lg[:, :, :], mx.unsqueeze(2).to_broadcast([P, T, NE]), ALU.subtract))
            v.wait_ge(r_exp, 1)
            step(v.tensor_reduce(sm, te(rt[1][:, :]), X, ALU.add))
            step(v.reciprocal(pack[:, :, 2], sm))
            step(v.tensor_scalar(rt[2][:, :], rt[0][:, :], 0.0, None, ALU.is_equal))
            step(v.tensor_tensor(te(rt[3][:, :]), te(rt[2][:, :]), wts.unsqueeze(1).to_broadcast([P, T, NE]), ALU.mult))
            step(v.tensor_reduce(fw, te(rt[3][:, :]), X, ALU.max))
            step(v.tensor_tensor(te(rt[2][:, :]), te(rt[3][:, :]), fw.unsqueeze(2).to_broadcast([P, T, NE]), ALU.is_equal))
            v.wait_ge(r_mm, 1)
            step(v.tensor_copy(rt[3][:, :].rearrange("p (e t) -> p e t", e=NE), te(bank[5][0:P, 0:T * NE]).rearrange("p t e -> p e t")))
            step(v.tensor_tensor_scan(rt[4][:, :], reset, rt[3][:, :], 0.0, ALU.mult, ALU.add))
            step(v.tensor_tensor(rt[3][:, :], rt[4][:, :], rt[3][:, :], ALU.subtract))
            n_e = rs[0][:, 0:8]
            step(v.tensor_scalar(n_e, rt[4][:, :].rearrange("p (e t) -> p e t", e=NE)[:, :, T - 1], 127.0, None, ALU.add))
            step(v.tensor_copy(rsi[:, :], n_e))
            step(v.tensor_scalar(rsi[:, :], rsi[:, :], 7, None, ALU.arith_shift_right))
            step(v.tensor_copy(n_e, rsi[:, :]))
            step(v.tensor_tensor_scan(rs[1][:, 0:8], reset[:, 1:9], n_e, 0.0, ALU.mult, ALU.add))
            step(v.tensor_tensor(rs[2][:, 0:8], rs[1][:, 0:8], n_e, ALU.subtract))
            step(v.tensor_scalar(rs[2][:, 0:8], rs[2][:, 0:8], 128.0, None, ALU.mult))
            step(v.tensor_tensor(rt[3][:, :].rearrange("p (e t) -> p e t", e=NE), rt[3][:, :].rearrange("p (e t) -> p e t", e=NE),
                                 rs[2][:, 0:8].unsqueeze(2).to_broadcast([P, NE, T]), ALU.add))
            step(v.tensor_tensor(te(rt[5][:, :]), te(bank[4][0:P, 0:T * NE]), rt[3][:, :].rearrange("p (e t) -> p t e", e=NE), ALU.add))
            step(v.tensor_tensor(rt[5][:, :], rt[5][:, :], rt[2][:, :], ALU.mult))
            step(v.tensor_reduce(pos, te(rt[5][:, :]), X, ALU.add))
            step(v.tensor_copy(pos_i[:, :], pos))
            step(v.tensor_copy(pack[:, :, 3].bitcast(I32), tok))
            ej = ejt[0:1, :].rearrange("p (j e) -> p j e", e=NE)
            step(v.tensor_tensor(ej, rs[1][0:1, 0:8].unsqueeze(1).to_broadcast([1, 64, NE]), jrow.unsqueeze(2).to_broadcast([1, 64, NE]), ALU.is_le))
            step(v.tensor_reduce(rs[0][0:1, :], ej, X, ALU.add))
            step(v.tensor_scalar(rs[0][0:1, :], rs[0][0:1, :], float(NE - 1), None, ALU.min))
            v.tensor_copy(e_row[:, :], rs[0][0:1, :]).then_inc(route_ready, 1)

            def d_pack(i):
                for u in range(2):
                    wait(v, scattered[u], 16 * i)
                    v.tensor_copy(srow[u][:, C:SROW], pack[:, ds(2 * i + u, 1), :].rearrange("p t c -> p (t c)")).then_inc(srow_ready[u], 1)

            pipelined(v, SB, [(0, d_pack)])
            v.wait_ge(route_ready, 1)
            for u in range(2):
                v.wait_ge(scattered[u], 16 * SB)

            def x_xn(i):
                for u in range(2):
                    v.wait_ge(xg_in[u], 16 * i + 16)
                    wait(v, gT_done, i)
                    v.tensor_scalar(xgn[u][:, :], xg[u][:, 0:C], xg[u][:, C:C + 1], xg[u][:, C + 1:C + 2], ALU.subtract, ALU.mult).then_inc(xgn_ready, 1)

            def x_out(i):
                for u in range(2):
                    v.wait_ge(y_ready, 2 * i + u + 1)
                    wait(v, out_stored[u], 16 * i)
                    v.scalar_tensor_tensor(og[u][:, :], bank[3 + u][:, 0:C], xg[u][:, C + 2:C + 3], xg[u][:, 0:C], ALU.mult, ALU.add).then_inc(og_ready, 1)

            pipelined(v, NT2 // 2, [(1, x_out), (0, x_xn)])


def kernel(x, src, dst, edge_attr_3, L0_gnn_W, L0_gnn_a_src, L0_gnn_a_dst, L0_gnn_edge_W, L0_gnn_edge_b, **w):
    import numpy as np
    import concourse.bacc as _bacc
    import concourse.mybir as _mybir
    from concourse.bass_utils import run_bass_kernel_spmd as _run

    f32, i32 = np.float32, np.int32

    def f(a):
        return np.asarray(a, f32)

    def rows(a):
        a = f(a)
        return a.reshape(-1, 128, a.shape[-1]).transpose(1, 0, 2)

    def cols(a):
        return f(a).reshape(-1, 128).T

    def all_rows(a, n):
        return np.broadcast_to(f(a), (n, np.size(a)))

    W = f(L0_gnn_W)
    abd = np.zeros((C, 16), f32)
    for h in range(H):
        abd[h * D:(h + 1) * D, h] = f(L0_gnn_a_src)[h]
        abd[h * D:(h + 1) * D, H + h] = f(L0_gnn_a_dst)[h]
    src_p, dst_p = np.zeros(EP, i32), np.full(EP, PAD_NODE, i32)
    src_p[:E], dst_p[:E] = np.asarray(src, i32), np.asarray(dst, i32)
    attr = np.zeros((3, EP), f32)
    attr[:, :E] = f(edge_attr_3).T
    ew, ewm = np.zeros((32, C), f32), np.zeros((32, 3), f32)
    for q, (_, part) in enumerate(COMBO):
        ew[3 * q:3 * q + 3] = f(L0_gnn_edge_W).T
        ewm[3 * q:3 * q + 3, part] = 1
    for part in range(3):
        ew[24 + part] = f(L0_gnn_edge_b)
        ewm[24 + part, part] = 1
    thr = np.zeros((64, 3), f32)
    thr[:, 0], thr[:, 1] = P * np.arange(64), 1e6
    thr[1:T, 1], thr[1:T, 2] = np.arange(1, T), 1
    kvm = np.zeros((128, 132), f32)
    for g in range(4):
        kvm[g * D:(g + 1) * D, g * D:(g + 1) * D] = 1
        kvm[g * D:(g + 1) * D, 128 + g] = 1
    routec = np.zeros((128, 773), f32)
    routec[:, 0:P] = np.arange(128)[:, None] < np.arange(P)[None, :]
    routec[:, P:2 * P] = 1
    reset = np.ones((NE, T), f32)
    reset[:, 0] = 0
    routec[:, 250:650] = reset.reshape(-1)
    routec[:, 650:658] = NE - np.arange(NE)
    routec[:, 658:722] = np.arange(64)
    token = np.arange(128)[:, None] + P * np.arange(T)[None, :]
    routec[:, 723:773] = token

    data = {
        "x": f(x),
        "wg": rows(W), "abd": rows(abd), "wgT": rows(W.T),
        "wkv": rows(np.concatenate([f(w["L0_mix_Wk"]), f(w["L0_mix_Wv"])], 1)),
        "bkv": all_rows(np.concatenate([f(w["L0_mix_bk"]), f(w["L0_mix_bv"])]), P),
        "attr": attr, "dst": dst_p,
        "dst_last": dst_p.reshape(1, NS, SE)[:, :, SE - 1],
        "dst_t": dst_p.reshape(NCH, 128).T, "src_t": src_p.reshape(NCH, 128).T,
        "ident": np.eye(128, dtype=f32), "nid": f(token), "eps": np.full((128, 1), EPS, f32),
        "ew": ew, "ewm": ewm, "thr": thr, "iota_items": np.arange(ITP, dtype=f32),
        "wq": rows(w["L0_mix_Wq"]), "bq": cols(w["L0_mix_bq"]), "wo": rows(w["L0_mix_Wo"]),
        "vec": np.stack([all_rows(w[n], 128) for n in VECS], 1), "kvm": kvm,
        "b1m": cols(w["L0_mix_b1"]), "w1m": rows(w["L0_mix_W1"]), "w2m": rows(w["L0_mix_W2"]),
        "node_row": np.arange(N, dtype=f32),
        "b1f": cols(w["L0_ffn_b1"]), "w1f": rows(w["L0_ffn_W1"]), "wgate": rows(w["L0_ffn_Wg"]),
        "bd": f(w["L0_ffn_bd"]).reshape(1, -1), "ones": np.ones((1, 128), f32), "bg": all_rows(w["L0_ffn_bg"], P),
        "routec": routec,
        "wd": f(w["L0_ffn_Wd"]).reshape(NE, JF, 128, C).transpose(2, 0, 1, 3).reshape(128, NE, JF * C),
    }
    data = {n: np.ascontiguousarray(a) for n, a in data.items()}
    nc = _bacc.Bacc("TRN2", target_bir_lowering=False, num_devices=1)
    io = {n: nc.dram_tensor(f"{n}_in", a.shape, _mybir.dt.from_np(a.dtype), kind="ExternalInput").ap() for n, a in data.items()}
    io["out"] = nc.dram_tensor("out_0_dram", (N, C), _mybir.dt.from_np(np.dtype(f32)), kind="ExternalOutput").ap()
    build_program(nc, io)
    r = _run(nc, [{f"{n}_in": a for n, a in data.items()}], core_ids=[0])
    return r.results[0]["out_0_dram"]
```
